# Optimizing a Trainium2 kernel written in Bass

```python
import numpy as np
import jax
import jax.numpy as jnp

def _softmax(x, axis=-1):
    return jax.nn.softmax(x, axis=axis)

def _gelu(x):
    return jax.nn.gelu(x, approximate=True)

def _silu(x):
    return jax.nn.silu(x)

def _sigmoid(x):
    return jax.nn.sigmoid(x)

def _layernorm(x, axis=-1, eps=1e-05):
    m = jnp.mean(x, axis=axis, keepdims=True)
    v = jnp.var(x, axis=axis, keepdims=True)
    return (x - m) / jnp.sqrt(v + eps)

def _scatter_add(tgt, idx, src, axis=0):
    return tgt.at[idx].add(src)

def _segment_sum(src, seg, n):
    return jax.ops.segment_sum(src, seg, n)
kernel_name = 'mk_prb_d2_jaxref_r8_1b3f9f'

def setup_inputs(seed: int=0):
    np.random.seed(seed)
    _w = jnp.asarray

    def _L0_attn_setup():
        import jax, jax.numpy as jnp
        import numpy as np
        DIM = 256
        SEGMENT_LEN = 128
        HEADS = 32
        DIM_HEAD = 64
        P = 16
        SCALE = 1.0 / np.sqrt(DIM_HEAD)
        key = jax.random.key(seed)
        ks = jax.random.split(key, 4)
        seq = jax.random.normal(ks[0], (2, 1024, DIM), dtype=jnp.float32)
        w_norm = jnp.ones((DIM,), dtype=jnp.float32)
        w_qkv = jax.random.normal(ks[1], (DIM, 3 * HEADS * DIM_HEAD), dtype=jnp.float32) * 0.02
        w_out = jax.random.normal(ks[2], (HEADS * DIM_HEAD, DIM), dtype=jnp.float32) * 0.02
        pm = jax.random.normal(ks[3], (2, HEADS, P, DIM_HEAD), dtype=jnp.float32) * 0.02
        return {'seq': seq, 'w_norm': w_norm, 'w_qkv': w_qkv, 'w_out': w_out, 'pm': pm}
    _L0_attn_in = _L0_attn_setup()

    def _L0_ffn_setup():
        import jax, jax.numpy as jnp
        import numpy as np
        LN_EPS = 1e-05
        Q_EPS = 1e-05

        def ternary_quantize(w):
            scale = jnp.mean(jnp.abs(w))
            return jnp.clip(jnp.round(w / (scale + Q_EPS)), -1.0, 1.0)

        def layernorm(x, gamma, beta):
            mu = jnp.mean(x, axis=-1, keepdims=True)
            var = jnp.mean(jnp.square(x - mu), axis=-1, keepdims=True)
            return (x - mu) * jax.lax.rsqrt(var + LN_EPS) * gamma + beta
        key = jax.random.key(seed)
        k_x, k_w = jax.random.split(key)
        B, S, D_IN, D_OUT = (4, 256, 256, 256)
        x = jax.random.normal(k_x, (B, S, D_IN), dtype=jnp.float32)
        std = np.sqrt(2.0 / D_OUT).astype(np.float32)
        weight = jax.random.normal(k_w, (D_OUT, D_IN), dtype=jnp.float32) * std
        bias = jnp.zeros((D_OUT,), dtype=jnp.float32)
        ln_gamma = jnp.ones((D_IN,), dtype=jnp.float32)
        ln_beta = jnp.zeros((D_IN,), dtype=jnp.float32)
        return {'x': x, 'weight': weight, 'bias': bias, 'ln_gamma': ln_gamma, 'ln_beta': ln_beta}
    _L0_ffn_in = _L0_ffn_setup()

    def _L1_attn_setup():
        import jax, jax.numpy as jnp
        import numpy as np
        HIDDEN = 256
        HQ = 32
        HKV = 4
        D = 64
        THETA = 10000.0
        SEQ = 256

        def _rope(x, pos):
            d = x.shape[-1]
            inv = 1.0 / THETA ** (jnp.arange(0, d, 2, dtype=jnp.float32) / d)
            ang = pos[:, None] * inv
            cos = jnp.cos(ang)[None, :, None, :]
            sin = jnp.sin(ang)[None, :, None, :]
            x1, x2 = jnp.split(x, 2, axis=-1)
            return jnp.concatenate([x1 * cos - x2 * sin, x2 * cos + x1 * sin], axis=-1)
        key = jax.random.key(seed)
        k1, k2, k3 = jax.random.split(key, 3)
        hidden_states = jax.random.normal(k1, (1, SEQ, HIDDEN), jnp.float32)
        w_qkv = jax.random.normal(k2, ((HQ + 2 * HKV) * D, HIDDEN), jnp.float32) * 0.02
        w_o = jax.random.normal(k3, (HIDDEN, HQ * D), jnp.float32) * 0.02
        return {'hidden_states': hidden_states, 'w_qkv': w_qkv, 'w_o': w_o}
    _L1_attn_in = _L1_attn_setup()

    def _L1_ffn_setup():
        import jax, jax.numpy as jnp
        import numpy as np
        EPS = 1e-06
        Q_B = 128.0

        def layer_norm(x):
            mean = jnp.mean(x, axis=-1, keepdims=True)
            var = jnp.var(x, axis=-1, keepdims=True)
            return (x - mean) / jnp.sqrt(var + EPS)

        def absmax_quant(x):
            gamma = jnp.max(jnp.abs(x), axis=-1, keepdims=True)
            x_hat = jnp.clip(x * Q_B / gamma, -Q_B + EPS, Q_B - EPS)
            return x_hat * gamma / Q_B

        def ternarize_weights(w):
            gamma = jnp.mean(jnp.abs(w))
            return jnp.sign(jnp.round(w / (gamma + EPS))) * gamma

        def bitlinear(x, w):
            xn = layer_norm(x)
            x_hat = xn + jax.lax.stop_gradient(absmax_quant(xn) - xn)
            w_hat = w + jax.lax.stop_gradient(ternarize_weights(w) - w)
            return jnp.einsum('bsd,od->bso', x_hat, w_hat)
        key = jax.random.key(seed)
        k1, k2, k3 = jax.random.split(key, 3)
        B, S, D = (4, 256, 256)
        x = jax.random.normal(k1, (B, S, D), dtype=jnp.float32)
        w_fc = jax.random.normal(k2, (4 * D, D), dtype=jnp.float32) / np.sqrt(D)
        w_proj = jax.random.normal(k3, (D, 4 * D), dtype=jnp.float32) / np.sqrt(4 * D)
        return {'x': x, 'w_fc': w_fc, 'w_proj': w_proj}
    _L1_ffn_in = _L1_ffn_setup()
    _d = {'L0_attn_seq': _L0_attn_in['seq'], 'L0_attn_w_norm': _L0_attn_in['w_norm'], 'L0_attn_w_qkv': _L0_attn_in['w_qkv'], 'L0_attn_w_out': _L0_attn_in['w_out'], 'L0_attn_pm': _L0_attn_in['pm'], 'L0_ffn_weight': _L0_ffn_in['weight'], 'L0_ffn_bias': _L0_ffn_in['bias'], 'L0_ffn_ln_gamma': _L0_ffn_in['ln_gamma'], 'L0_ffn_ln_beta': _L0_ffn_in['ln_beta'], 'L1_attn_w_qkv': _L1_attn_in['w_qkv'], 'L1_attn_w_o': _L1_attn_in['w_o'], 'L1_ffn_w_fc': _L1_ffn_in['w_fc'], 'L1_ffn_w_proj': _L1_ffn_in['w_proj']}
    _x0 = _d['L0_attn_seq']
    _d['L0_attn_seq'] = jax.random.normal(jax.random.fold_in(jax.random.key(seed), 1), (4, 256, 256), dtype=_x0.dtype)
    del _x0
    return _d

def reference(L0_attn_seq, L0_attn_w_norm, L0_attn_w_qkv, L0_attn_w_out, L0_attn_pm, L0_ffn_weight, L0_ffn_bias, L0_ffn_ln_gamma, L0_ffn_ln_beta, L1_attn_w_qkv, L1_attn_w_o, L1_ffn_w_fc, L1_ffn_w_proj):

    def _L0_attn_ref(seq, w_norm, w_qkv, w_out, pm):
        import jax, jax.numpy as jnp
        import numpy as np
        DIM = 256
        SEGMENT_LEN = 128
        HEADS = 32
        DIM_HEAD = 64
        P = 16
        SCALE = 1.0 / np.sqrt(DIM_HEAD)
        b, seq_len, d = seq.shape
        next_len = -(-seq_len // SEGMENT_LEN) * SEGMENT_LEN
        pad = next_len - seq_len
        x = jnp.pad(seq, ((0, 0), (0, pad), (0, 0))) if pad > 0 else seq
        w = next_len // SEGMENT_LEN
        x = x.reshape(b * SEGMENT_LEN, w, d)
        eps = jnp.finfo(x.dtype).eps
        x = x * jax.lax.rsqrt(jnp.mean(jnp.square(x), axis=-1, keepdims=True) + eps) * w_norm
        qkv = x @ w_qkv
        q, k, v = jnp.split(qkv, 3, axis=-1)
        B = x.shape[0]
        split = lambda t: t.reshape(B, w, HEADS, DIM_HEAD).transpose(0, 2, 1, 3)
        q, k, v = (split(q), split(k), split(v))
        pmk = jnp.broadcast_to(pm[0], (B, HEADS, P, DIM_HEAD))
        pmv = jnp.broadcast_to(pm[1], (B, HEADS, P, DIM_HEAD))
        k = jnp.concatenate([pmk, k], axis=2)
        v = jnp.concatenate([pmv, v], axis=2)
        scores = jnp.einsum('bhqd,bhkd->bhqk', q, k) * SCALE
        mask = jnp.arange(P + w)[None, :] <= jnp.arange(w)[:, None]
        scores = jnp.where(mask, scores, jnp.finfo(scores.dtype).min)
        attn = jax.nn.softmax(scores, axis=-1)
        out = jnp.einsum('bhqk,bhkd->bhqd', attn, v)
        out = out.transpose(0, 2, 1, 3).reshape(B, w, HEADS * DIM_HEAD)
        out = out @ w_out
        out = out.reshape(b, SEGMENT_LEN * w, d)
        return out[:, :seq_len]

    def _L0_ffn_ref(x, weight, bias, ln_gamma, ln_beta):
        import jax, jax.numpy as jnp
        import numpy as np
        LN_EPS = 1e-05
        Q_EPS = 1e-05

        def ternary_quantize(w):
            scale = jnp.mean(jnp.abs(w))
            return jnp.clip(jnp.round(w / (scale + Q_EPS)), -1.0, 1.0)

        def layernorm(x, gamma, beta):
            mu = jnp.mean(x, axis=-1, keepdims=True)
            var = jnp.mean(jnp.square(x - mu), axis=-1, keepdims=True)
            return (x - mu) * jax.lax.rsqrt(var + LN_EPS) * gamma + beta
        xn = layernorm(x, ln_gamma, ln_beta)
        w_q = ternary_quantize(weight)
        return jnp.einsum('bsi,oi->bso', xn, w_q) + bias

    def _L1_attn_ref(hidden_states, w_qkv, w_o):
        import jax, jax.numpy as jnp
        import numpy as np
        HIDDEN = 256
        HQ = 32
        HKV = 4
        D = 64
        THETA = 10000.0
        SEQ = 256

        def _rope(x, pos):
            d = x.shape[-1]
            inv = 1.0 / THETA ** (jnp.arange(0, d, 2, dtype=jnp.float32) / d)
            ang = pos[:, None] * inv
            cos = jnp.cos(ang)[None, :, None, :]
            sin = jnp.sin(ang)[None, :, None, :]
            x1, x2 = jnp.split(x, 2, axis=-1)
            return jnp.concatenate([x1 * cos - x2 * sin, x2 * cos + x1 * sin], axis=-1)
        b, s, _ = hidden_states.shape
        qkv = jnp.einsum('bsh,oh->bso', hidden_states, w_qkv).reshape(b, s, HQ + 2 * HKV, D)
        q = qkv[:, :, :HQ]
        k = qkv[:, :, HQ:HQ + HKV]
        v = qkv[:, :, HQ + HKV:]
        pos = jnp.arange(s, dtype=jnp.float32)
        q = _rope(q, pos)
        k = _rope(k, pos)
        rep = HQ // HKV
        k = jnp.repeat(k, rep, axis=2)
        v = jnp.repeat(v, rep, axis=2)
        scores = jnp.einsum('bqhd,bkhd->bhqk', q, k) * D ** (-0.5)
        causal = jnp.tril(jnp.ones((s, s), dtype=bool))
        scores = jnp.where(causal[None, None], scores, jnp.finfo(scores.dtype).min)
        attn = jax.nn.softmax(scores, axis=-1)
        out = jnp.einsum('bhqk,bkhd->bqhd', attn, v).reshape(b, s, HQ * D)
        return jnp.einsum('bso,ho->bsh', out, w_o)

    def _L1_ffn_ref(x, w_fc, w_proj):
        import jax, jax.numpy as jnp
        import numpy as np
        EPS = 1e-06
        Q_B = 128.0

        def layer_norm(x):
            mean = jnp.mean(x, axis=-1, keepdims=True)
            var = jnp.var(x, axis=-1, keepdims=True)
            return (x - mean) / jnp.sqrt(var + EPS)

        def absmax_quant(x):
            gamma = jnp.max(jnp.abs(x), axis=-1, keepdims=True)
            x_hat = jnp.clip(x * Q_B / gamma, -Q_B + EPS, Q_B - EPS)
            return x_hat * gamma / Q_B

        def ternarize_weights(w):
            gamma = jnp.mean(jnp.abs(w))
            return jnp.sign(jnp.round(w / (gamma + EPS))) * gamma

        def bitlinear(x, w):
            xn = layer_norm(x)
            x_hat = xn + jax.lax.stop_gradient(absmax_quant(xn) - xn)
            w_hat = w + jax.lax.stop_gradient(ternarize_weights(w) - w)
            return jnp.einsum('bsd,od->bso', x_hat, w_hat)
        h = bitlinear(x, w_fc)
        h = jax.nn.gelu(h, approximate=False)
        return bitlinear(h, w_proj)
    x = L0_attn_seq
    xn = _layernorm(x, axis=-1)
    x = x + _L0_attn_ref(xn, L0_attn_w_norm, L0_attn_w_qkv, L0_attn_w_out, L0_attn_pm) + _L0_ffn_ref(xn, L0_ffn_weight, L0_ffn_bias, L0_ffn_ln_gamma, L0_ffn_ln_beta)
    xn = _layernorm(x, axis=-1)
    x = x + _L1_attn_ref(xn, L1_attn_w_qkv, L1_attn_w_o) + _L1_ffn_ref(xn, L1_ffn_w_fc, L1_ffn_w_proj)
    return x

_drawn_inputs = setup_inputs


def setup_inputs(seed=0):
    import zlib

    import numpy as np

    out = dict(_drawn_inputs(seed))
    spreads = {'L0_attn_w_norm': (1.0, 0.6),
     'L0_ffn_bias': (0.0, 0.8),
     'L0_ffn_ln_gamma': (1.0, 0.2),
     'L0_ffn_ln_beta': (0.0, 0.1)}
    factors = {'L0_attn_w_qkv': 8.0,
     'L0_attn_w_out': 8.0,
     'L0_attn_pm': 8.0,
     'L1_attn_w_qkv': 8.0,
     'L1_attn_w_o': 8.0}
    for name, (base, spread) in spreads.items():
        noise = np.random.default_rng([zlib.crc32(name.encode()), seed]).standard_normal(out[name].shape)
        drawn = base * np.exp(spread * noise) if base else spread * noise
        out[name] = jnp.asarray(drawn.astype(out[name].dtype))
    for name, factor in factors.items():
        out[name] = (out[name] * factor).astype(out[name].dtype)
    return out
```

```python
from contextlib import ExitStack

import numpy as np

import concourse.bass as bass
from concourse import mybir

F32 = mybir.dt.float32
F32R = mybir.dt.float32r
BF16 = mybir.dt.bfloat16
ALU = mybir.AluOpType
ACT = mybir.ActivationFunctionType
AX = mybir.AxisListType

P = 128
B, SEQ, DIM = 4, 256, 256
KC = DIM // P
H, DH = 32, 64
HKV = 4
HG = H // HKV
HC = H * DH // P
QKV1 = (H + 2 * HKV) * DH
FF = 4 * DIM
THETA = 10000.0
EPS_LN, EPS_BIT = 1e-5, 1e-6
EPS_RMS = float(np.finfo(np.float32).eps)
MAGIC = 1.5 * 2.0 ** 23
MASKED = -1e30
RING = 6
ITS = B * HKV
UNITS = 6

C_ID, C_MASK, C_EVEN, C_ONE, C_QC, C_QS, C_KC, C_KS = (P * i for i in range(8))
C_ALL = 8 * P


def constants():
    c = np.zeros((P, C_ALL), np.float32)
    c[:, C_ID:C_ID + P] = np.eye(P)
    c[:, C_MASK:C_MASK + P] = np.where(np.arange(P)[None] > np.arange(P)[:, None], MASKED, 0.0)
    c[0:2 * H:2, C_EVEN:C_EVEN + P] = 1.0
    c[:, C_ONE:C_ONE + P] = 1.0
    inv = (1.0 / np.float32(THETA) ** (np.arange(0, DH, 2, dtype=np.float32) / np.float32(DH))).astype(np.float32)
    for t in range(2):
        ang = (np.arange(P, dtype=np.float32) + np.float32(P * t))[:, None] * inv[None]
        cos = np.cos(ang).astype(np.float32)
        sin = np.sin(ang).astype(np.float32)
        cc, ss = np.concatenate([cos, cos], 1), np.concatenate([-sin, sin], 1)
        at = DH * t
        c[:, C_QC + at:C_QC + at + DH] = cc * np.float32(DH ** -0.5)
        c[:, C_QS + at:C_QS + at + DH] = ss * np.float32(DH ** -0.5)
        c[:, C_KC + at:C_KC + at + DH] = cc
        c[:, C_KS + at:C_KS + at + DH] = ss
    return c


ORDER = ([("yT0", b) for b in range(B)] + [("ffn0T", 0)] + [("wq0T", j) for j in range(HC // 2)]
         + [("score0", 0)] + [("qkvT", j) for j in range(QKV1 // 256)] + [("probT0", 0)]
         + [("out0", b) for b in range(B)] + [("woT", j) for j in range(HC // 2)]
         + [("fcT", j) for j in range(FF // 256)] + [("projT", j) for j in range(FF // 256)]
         + [("yT1", b) for b in range(B)])
UNIT = {key: n for n, key in enumerate(ORDER)}
RELEASES = {"yT0": "act", "ffn0T": "act", "wq0T": "dve", "score0": "dve", "qkvT": "dve", "probT0": "act",
            "out0": "dve", "woT": "act", "fcT": "act", "projT": "act", "yT1": "dve"}


def released(engine, n):
    return sum(RELEASES[what] == engine for what, _ in ORDER[:n + 1])


def build(nc, seq, w_qkv0, w_out0, pm, w_ffn0, bias0, w_qkv1, w_o1, w_fc, w_proj, vec, const, out):
    with ExitStack() as ctx:
        def sb(name, shape, dt=F32):
            return ctx.enter_context(nc.sbuf_tensor(name, shape, dt))

        def sem(name):
            return ctx.enter_context(nc.semaphore(name))

        bank = [ctx.enter_context(nc.psum_tensor(f"bank{i}", [P, 512], F32)) for i in range(8)]

        cst = sb("cst", [P, C_ALL])
        ident = cst[:, C_ID:C_ID + P]
        ident_b = sb("ident_b", [P, P], BF16)
        mask_b = sb("mask_b", [P, 4, P], BF16)
        x = sb("x", [P, B, 2, DIM])
        stats = sb("stats", [P, 8, 6])
        mv = sb("mv", [P, 8, 2])
        tok = sb("tok", [P, 8, 8])
        vecs = sb("vecs", [P, 3, KC])
        bias_row = sb("bias_row", [1, DIM])
        pmn = sb("pmn", [H, 2, 2, 2, DH])
        blk_k = sb("blk_k", [P, HC, 2, 2])
        blk_v = sb("blk_v", [P, HC * 68])
        g0 = sb("g0", [P, KC, 2 * H])
        m0 = sb("m0", [2 * H, DIM])
        neg_half = sb("neg_half", [P, 8])
        wsum = sb("wsum", [P, 4])
        wscale = sb("wscale", [P, 4])
        small = sb("small", [P, 4, 2 * H * B])
        probT0 = sb("probT0", [2 * H, B * P])
        xrT = sb("xrT", [P, KC, B * P])

        wq0 = sb("wq0", [P, KC * 2048])
        wo_t = sb("wo_t", [P, HC, DIM])
        nat_qkv = sb("nat_qkv", [P, QKV1 // P, DIM])
        nat_o = sb("nat_o", [P, 2, H * DH])
        nat_fc = sb("nat_fc", [P, FF // P, DIM])
        nat_proj = sb("nat_proj", [P, 2, FF])
        nat_ffn0 = sb("nat_ffn0", [P, 2, DIM])

        qkvT = [sb(f"qkvT_{s}", [P, KC, QKV1], F32R) for s in ("hi", "lo")]
        xT = [sb(f"xT_{s}", [P, KC, B * SEQ], F32R) for s in ("hi", "lo")]
        fcT = sb("fcT", [P, KC, FF], F32R)
        projT = sb("projT", [P, FF // P, DIM], F32R)
        ffn0T = sb("ffn0T", [P, KC, DIM], F32R)
        qT = sb("qT", [P, HG, SEQ], F32R)
        hT_lo = sb("hT_lo", [P, FF // P, P], F32R)
        kT = sb("kT", [P, 2, SEQ], F32R)
        hT = [qT[:, 0:4, :].rearrange("p a (b t) -> p (a b) t", b=2), hT_lo[:, :, :]]
        xb = [hT_lo[:, 0:4, :], hT_lo[:, 4:8, :]]

        y0 = nat_proj[:, :, :].rearrange("p a b -> p (a b)").rearrange("p (b e d) -> p b e d", b=B, e=2)
        y1 = wq0[:, 0:2048].rearrange("p (b e d) -> p b e d", b=B, e=2)
        ffn_h = wq0[:, 2048:4096].rearrange("p (s n) -> p s n", s=2)
        flat_q = nat_qkv[:, :, :].rearrange("p a b -> p (a b)")
        flat_o = nat_o[:, :, :].rearrange("p a b -> p (a b)")
        flat_f = nat_fc[:, :, :].rearrange("p a b -> p (a b)")
        flat_p = nat_proj[:, :, :].rearrange("p a b -> p (a b)")
        prob = [flat_q[:, 512 * i:512 * i + 512] for i in range(3)]
        probT = [flat_q[:, 512 * (3 + i):512 * (3 + i) + 512] for i in range(3)]
        o_n = flat_q[:, 3072:4096].rearrange("p (c n) -> p c n", c=2)
        oT = flat_q[:, 4096:5120].rearrange("p (c t) -> p c t", c=4)
        q_nat = flat_o[:, 0:2048].rearrange("p (c h s d) -> p c h s d", c=2, h=HG, s=2)
        rope_a = flat_o[:, 2048:3072].rearrange("p (c n) -> p c n", c=2)
        rope_b = flat_o[:, 3072:4096].rearrange("p (c n) -> p c n", c=2)
        k_nat = flat_f[:, 0:512].rearrange("p (c s w d) -> p s c w d", s=2, c=2, w=2)
        rope_k = flat_f[:, 512:768].rearrange("p (s c d) -> p s c d", s=2, c=2)
        v_stage = flat_f[:, 768:896].rearrange("p (c d) -> p c d", c=2)
        v = flat_f[:, 896:1024].rearrange("p (c d) -> p c d", c=2)
        neg_max = flat_f[:, 1024:1040]
        sums = flat_f[:, 1040:1056]
        rsum = flat_f[:, 1056:1072]
        fstat = flat_f[:, 1072:1072 + 8 * 12].rearrange("p (t n) -> p t n", t=8)
        fmv = flat_f[:, 1200:1216].rearrange("p (t n) -> p t n", t=8)
        ffac = flat_f[:, 1216:1216 + 64].rearrange("p (t n) -> p t n", t=8)
        yT_full = flat_o[:, 0:2048].rearrange("p (b n) -> p b n", b=B)
        wq0T = flat_o[:, 2048:4096].rearrange("p (s n) -> p s n", s=4)

        ld = {n: sem("ld_" + n) for n in ("x", "cst", "vec", "pm", "ffn0", "wq0", "wout", "qkv", "o", "fc", "proj")}
        s_dve, s_pool = sem("s_dve"), sem("s_pool")
        filled = sem("filled")
        rel = {"act": sem("rel_act"), "dve": sem("rel_dve")}
        hi_done = sem("hi_done")
        const_done = sem("const_done")
        y_done = sem("y_done")
        y1_done = sem("y1_done")
        sum0_in, sum0_out = sem("sum0_in"), sem("sum0_out")
        sum1_in, sum1_out = sem("sum1_in"), sem("sum1_out")
        tern0, tern1 = sem("tern0"), sem("tern1")
        full_done = sem("full_done")
        xrT_done = sem("xrT_done")
        lo0_done = sem("lo0_done")
        blk_zero, pm_full, blk_done = sem("blk_zero"), sem("pm_full"), sem("blk_done")
        g_mm, g_done = sem("g_mm"), sem("g_done")
        m_full, m_done = sem("m_full"), sem("m_done")
        e_in, e_out, prob0 = sem("e_in"), sem("e_out"), sem("prob0")
        f_fc, f_gelu, f_y, f_T, f_hi, f_lo, f_out, f_add = (sem("f_" + n) for n in
                                                            ("fc", "gelu", "y", "T", "hi", "lo", "out", "add"))
        xb_done = sem("xb_done")
        full6, free6, full7, free7 = sem("full6"), sem("free6"), sem("full7"), sem("free7")
        qn_done, kn_done, v_done = sem("qn_done"), sem("kn_done"), sem("v_done")
        s_full, s_max, s_exp, t_full, t_done, pv_done = (sem(n) for n in
                                                         ("s_full", "s_max", "s_exp", "t_full", "t_done", "pv_done"))
        rs_done, normed = sem("rs_done"), sem("normed")
        f_fac, root_in, root_out = sem("f_fac"), sem("root_in"), sem("root_out")
        stored = sem("stored")
        block = ctx.enter_context(nc.Block())

        def chained(engine, own):
            count = [0]

            def link(ins):
                count[0] += 1
                ins.then_inc(own, 1)
                engine.wait_ge(own, count[0])
            return link

        SIX = {"oT0": 0, "oT1": 1, "wo0": 2, "wo1": 3, "qT1": 4, "qT3": 5}
        SEVEN = {"q0": 0, "q1": 1, "kv": 2, "qT0": 3, "qT2": 4, "kT": 5}

        def place(what, it, last=False):
            if what in SIX and it is -1:
                return bank[6], full6, free6, SIX[what] - 4
            if what in SIX:
                return bank[6], full6, free6, it * 6 - 2 + SIX[what] - (2 if last else 0)
            return bank[7], full7, free7, it * 6 + 6 + SEVEN[what]

        @block.sync
        def _(sp):
            sp.dma_start(x[:, :, :, :], seq.rearrange("b (p e) d -> p b e d", e=2)).then_inc(ld["x"], 16)
            sp.dma_start(cst[:, :], const).then_inc(ld["cst"], 16)
            sp.dma_start(nat_ffn0[:, :, :], w_ffn0.rearrange("(c p) i -> p c i", p=P)).then_inc(ld["ffn0"], 16)
            for w in range(2):
                for d in range(2):
                    sp.dma_start(pmn[:, w, :, d, :], pm[w, :, 0:2, :]).then_inc(ld["pm"], 16)
            sp.dma_start(wq0[:, :].rearrange("p (c n) -> p c n", c=KC),
                         w_qkv0.rearrange("(c p) n -> p c n", p=P)[:, :, 0:H * DH]).then_inc(ld["wq0"], 16)
            sp.dma_start(wo_t[:, :, :], w_out0.rearrange("(c p) n -> p c n", p=P)).then_inc(ld["wout"], 16)
            sp.dma_start(nat_qkv[:, :, :], w_qkv1.rearrange("(c p) n -> p c n", p=P)).then_inc(ld["qkv"], 16)
            sp.dma_start(nat_fc[:, :, :], w_fc.rearrange("(c p) n -> p c n", p=P)).then_inc(ld["fc"], 16)
            sp.wait_ge(filled, B)
            sp.dma_start(nat_proj[:, :, :], w_proj.rearrange("(c p) n -> p c n", p=P)).then_inc(ld["proj"], 16)
            sp.wait_ge(lo0_done, B)
            sp.wait_ge(g_mm, HC // 2)
            sp.dma_start(nat_o[:, :, :], w_o1.rearrange("(c p) n -> p c n", p=P)).then_inc(ld["o"], 16)
            sp.wait_ge(free6, ITS * 6 - 4 + 4)
            sp.dma_start(out.rearrange("b (p e) d -> p b e d", e=2), x[:, :, :, :]).then_inc(stored, 16)
            sp.wait_ge(stored, 16)

        @block.scalar
        def _(act):
            act.dma_start(vecs[:, :, :], vec).then_inc(ld["vec"], 16)
            act.dma_start(bias_row[:, :], bias0.rearrange("(a n) -> a n", a=1)).then_inc(ld["vec"], 16)

            def unit(what, j=0):
                n = UNIT[(what, j)]
                act.wait_ge(filled, n + 1)
                return bank[n % RING]

            act.wait_ge(ld["vec"], 32)
            for b in range(B):
                ps = unit("yT0", b)[:, :].rearrange("p (k e t) -> p k e t", k=KC, e=2)
                for k in range(KC):
                    ins = nc.scalar.activation(yT_full[:, b, 256 * k:256 * k + 256].rearrange("p (e t) -> p e t", e=2), ps[:, k, :, :],
                                               ACT.Identity, bias=vecs[:, 1, k:k + 1], scale=vecs[:, 0, k:k + 1])
                ins.then_inc(full_done, 1)
                for k in range(KC):
                    ins = nc.scalar.activation(xrT[:, k, P * b:P * b + P], ps[:, k, 1, :], ACT.Identity,
                                               scale=vecs[:, 2, k:k + 1])
                ins.then_inc(rel["act"], 1)
            ps = unit("ffn0T")
            nc.scalar.activation(ffn0T[:, :, :], ps[:, :].rearrange("p (k n) -> p k n", k=KC),
                                 ACT.Copy).then_inc(rel["act"], 1)
            act.wait_ge(e_in, 1)
            nc.scalar.activation(small[:, 1, :], small[:, 0, :], ACT.Exp).then_inc(e_out, 1)
            for j in range(QKV1 // 256):
                ps = unit("qkvT", j)
                nc.scalar.activation(qkvT[0][:, :, 256 * j:256 * j + 256], ps[:, :].rearrange("p (k n) -> p k n", k=KC),
                                     ACT.Copy).then_inc(hi_done, 1)
            ps = unit("probT0")
            nc.scalar.activation(probT0[:, :], ps[0:2 * H, :], ACT.Copy).then_inc(rel["act"], 1)
            act.wait_ge(m_full, 1)
            for j in range(HC // 2):
                ps = unit("woT", j)
                nc.scalar.activation(wo_t[:, 2 * j:2 * j + 2, :], ps[:, :].rearrange("p (k n) -> p k n", k=2),
                                     ACT.Copy).then_inc(rel["act"], 1)
            for j in range(FF // 256):
                ps = unit("fcT", j)
                nc.scalar.activation(fcT[:, :, 256 * j:256 * j + 256], ps[:, :].rearrange("p (k n) -> p k n", k=KC),
                                     ACT.Copy).then_inc(rel["act"], 1)
            for j in range(FF // 256):
                ps = unit("projT", j)
                nc.scalar.activation(projT[:, 2 * j:2 * j + 2, :], ps[:, :].rearrange("p (k n) -> p k n", k=2),
                                     ACT.Copy).then_inc(rel["act"], 1)
            for b in range(B):
                ps = unit("yT1", b)[:, :].rearrange("p (k e t) -> p k t e", k=KC, e=2)
                for k in range(KC):
                    ins = nc.scalar.activation(xT[0][:, k, SEQ * b:SEQ * b + SEQ].rearrange("p (t e) -> p t e", e=2),
                                               ps[:, k, :, :], ACT.Copy)
                ins.then_inc(hi_done, 1)

            def hidden_hi(t):
                if t >= 1:
                    act.wait_ge(f_out, t)
                for half in range(2):
                    act.wait_ge(f_T, 2 * t + half + 1)
                    nc.scalar.activation(hT[0][:, 4 * half:4 * half + 4, :],
                                         bank[4 + half][:, :].rearrange("p (k n) -> p k n", k=4),
                                         ACT.Copy).then_inc(f_hi, 1)

            act.wait_ge(f_fac, 1)
            for t in range(8):
                act.wait_ge(f_fc, t + 1)
                if t >= 2:
                    act.wait_ge(f_T, 2 * (t - 1))
                for half in range(2):
                    ins = nc.scalar.activation(ffn_h[:, t % 2, 512 * half:512 * half + 512],
                                               bank[2 * (t % 2) + half][:, :], ACT.Gelu, scale=ffac[:, t, 0:1])
                ins.then_inc(f_gelu, 1)
                if t >= 1:
                    hidden_hi(t - 1)
            hidden_hi(7)

            def hi_lo_T(what, it):
                ps, full, free, n = place(what, it)
                act.wait_ge(full, n + 1)
                if what == "kT":
                    dst = kT[:, :, :]
                    src = ps[:, :].rearrange("p (s t) -> p s t", s=2)
                else:
                    j = int(what[2])
                    c, h = j // 2, 4 * (j % 2)
                    dst = qT[:, h:h + 4, P * c:P * c + P]
                    src = ps[:, :].rearrange("p (h t) -> p h t", h=4)
                nc.scalar.activation(dst, src, ACT.Copy).then_inc(free, 1)

            def probs(it, u):
                n = it * UNITS + u
                act.wait_ge(s_max, n + 1)
                wide, heads = (P, 4) if u < 2 else (2 * P, 2)
                h = 4 * u if u < 2 else 8 + 2 * (u - 2)
                for j in range(heads):
                    ins = nc.scalar.activation(prob[u % 3][:, wide * j:wide * j + wide], bank[u % 2][:, wide * j:wide * j + wide],
                                               ACT.Exp, bias=neg_max[:, h + j:h + j + 1],
                                               accum_out=sums[:, h + j:h + j + 1])
                ins.then_inc(s_exp, 1)

            def probs_T(it, u):
                n = it * UNITS + u
                act.wait_ge(t_full, n + 1)
                nc.scalar.activation(probT[u % 3], bank[2 + u % 2][:, :], ACT.Copy).then_inc(t_done, 1)

            def heads_T(what, it, last=False):
                ps, full, free, n = place(what, it, last)
                act.wait_ge(full, n + 1)
                c = int(what[2])
                nc.scalar.activation(oT[:, :, P * c:P * c + P], ps[:, :].rearrange("p (c t) -> p c t", c=4),
                                     ACT.Copy).then_inc(free, 1)

            def iteration(it, first=False, last=False):
                for s in range(UNITS + 2):
                    if s < UNITS:
                        if not first and s in (0, 2):
                            act.wait_ge(normed, it * 2 - (1 if s == 0 else 0))
                        if s >= 3 or not first:
                            act.wait_ge(t_full, it * UNITS + s - 2)
                        probs(it, s)
                    if s == 0 and not first:
                        heads_T("oT0", it)
                    if s == 1 and not first:
                        heads_T("oT1", it)
                    if s >= 2:
                        u = s - 2
                        if u >= 3 or not first:
                            act.wait_ge(pv_done, it * UNITS + u - 2)
                        probs_T(it, u)
                if not last:
                    for what in ("qT0", "qT1", "qT2", "qT3", "kT"):
                        hi_lo_T(what, it)

            for what in ("qT0", "qT1", "qT2", "qT3", "kT"):
                hi_lo_T(what, -1)
            iteration(0, first=True)
            with act.Fori(1, ITS - 1) as it:
                iteration(it)
            iteration(ITS - 1, last=True)
            heads_T("oT0", ITS, last=True)
            heads_T("oT1", ITS, last=True)

        @block.gpsimd
        def _(pool):
            pool.memset(blk_k[:, :, :, :], 0.0).then_inc(blk_zero, 1)
            pool.memset(blk_v[:, :], 0.0).then_inc(blk_zero, 1)
            pool.memset(neg_half[:, :], -0.5).then_inc(blk_zero, 1)
            pool.wait_ge(blk_zero, 3)
            r, ms, c1, c2, rc, f1 = (tok[:, i, :] for i in range(6))
            for n, a in enumerate([r, c1, c2, r, c2] + [ffac[:, t, 1:2] for t in range(8)]):
                pool.wait_ge(root_in, n + 1)
                pool.tensor_tensor(a, a, neg_half[:, 0:a.shape[1]], ALU.pow).then_inc(root_out, 1)
            OWN = 3

            def own(ins, n):
                ins.then_inc(s_pool, 1)
                pool.wait_ge(s_pool, n)

            def sequence(it):
                for s in range(2):
                    ins = pool.tensor_copy(xb[s].rearrange("p (k c) t -> p k (c t)", k=KC),
                                           xT[s][:, :, bass.ds((it // HKV) * SEQ, SEQ)])
                ins.then_inc(xb_done, 1)

            def queries(it, n):
                for c in range(2):
                    pool.wait_ge(free7, place(f"q{c}", it)[3] + 1)
                    if c == 0 and it is not -1:
                        pool.wait_ge(full7, it * 6 + 6)
                    hi, lo = (q_nat[:, c, :, s, :] for s in range(2))
                    split = [a.rearrange("p (h d) -> p h d", h=HG) for a in (rope_a[:, c, :], rope_b[:, c, :])]
                    pool.tensor_tensor(hi.bitcast(F32R), *split, ALU.add)
                    own(pool.tensor_tensor(split[0], *split, ALU.add), n + c + 1)
                    pool.tensor_tensor(lo, split[0], hi, ALU.subtract).then_inc(qn_done, 1)

            def keys(it, n):
                pool.wait_ge(free7, place("kv", it)[3] + 1)
                a, b = rope_k[:, 0, :, :], rope_k[:, 1, :, :]
                for w in range(2):
                    pool.tensor_tensor(k_nat[:, 0, :, w, :].bitcast(F32R), a, b, ALU.add)
                own(pool.tensor_tensor(a, a, b, ALU.add), n + 3)
                for w in range(2):
                    ins = pool.tensor_tensor(k_nat[:, 1, :, w, :], a, k_nat[:, 0, :, w, :], ALU.subtract)
                ins.then_inc(kn_done, 1)

            pool.wait_ge(filled, len(ORDER))
            pool.wait_ge(rel["dve"], released("dve", len(ORDER) - 1))
            pool.wait_ge(f_out, 8)
            sequence(0)
            def iteration(it, more=True):
                queries(it, OWN * (it + 1))
                keys(it, OWN * (it + 1))
                if more:
                    sequence(it + 2)

            queries(-1, 0)
            keys(-1, 0)
            sequence(1)
            with pool.Fori(0, ITS - 2) as it:
                iteration(it)
            iteration(ITS - 2, more=False)

        @block.vector
        def _(dve):
            link = chained(dve, s_dve)

            def unit(what, j=0):
                n = UNIT[(what, j)]
                dve.wait_ge(filled, n + 1)
                return bank[n % RING]

            def layer_stats():
                for t in range(8):
                    ins = dve.bn_stats(stats[:, t, :], x[:, t // 2, t % 2, :])
                link(ins)
                for t in range(8):
                    ins = dve.bn_aggr(mv[:, t, :], stats[:, t, :])
                link(ins)

            roots = [0]

            def rsqrt(dst, src, eps):
                roots[0] += 1
                dve.tensor_scalar(dst, src, eps, None, ALU.add).then_inc(root_in, 1)
                dve.wait_ge(root_out, roots[0])

            r, ms, c1, c2, rc, f1 = (tok[:, i, :] for i in range(6))
            mean, var = mv[:, :, 0], mv[:, :, 1]

            dve.wait_ge(ld["x"], 16)
            layer_stats()
            rsqrt(r, var, EPS_LN)
            link(dve.tensor_tensor(ms, r, r, ALU.mult))
            link(dve.tensor_tensor(ms, ms, var, ALU.mult))
            rsqrt(c1, ms, EPS_RMS)
            rsqrt(c2, ms, EPS_LN)
            link(dve.tensor_tensor(rc, r, c2, ALU.mult))
            for t in range(8):
                ins = dve.tensor_scalar(y0[:, t // 2, t % 2, :], x[:, t // 2, t % 2, :], mean[:, t:t + 1], rc[:, t:t + 1],
                                        ALU.subtract, ALU.mult)
                if t % 2:
                    ins.then_inc(y_done, 1)
            link(dve.reciprocal(f1, c2))
            link(dve.tensor_tensor(f1, f1, c1, ALU.mult))
            link(dve.tensor_scalar(f1, f1, DH ** -0.5, None, ALU.mult))
            dve.wait_ge(ld["cst"], 16)
            dve.tensor_copy(ident_b[:, :], ident)
            for j in range(4):
                ins = dve.tensor_copy(mask_b[:, j, :], cst[:, C_MASK:C_MASK + P])
            ins.then_inc(const_done, 1)

            def ternary(w, scale):
                link(dve.tensor_scalar(w, w, scale, MAGIC, ALU.mult, ALU.add))
                link(dve.tensor_scalar(w, w, MAGIC, 1.0, ALU.subtract, ALU.min))
                return dve.tensor_scalar(w, w, -1.0, None, ALU.max)

            def magnitude(j, w):
                return dve.tensor_reduce(wsum[:, j:j + 1], w, AX.XY, ALU.add, apply_absolute_value=True)

            dve.wait_ge(ld["ffn0"], 16)
            magnitude(0, nat_ffn0[:, :, :]).then_inc(sum0_in, 1)
            dve.wait_ge(sum0_out, 1)
            link(dve.tensor_scalar(wscale[:, 0:1], bank[7][:, 0:1], 1.0 / (DIM * DIM), 1e-5, ALU.mult, ALU.add))
            link(dve.reciprocal(wscale[:, 0:1], wscale[:, 0:1]))
            ternary(nat_ffn0[:, :, :], wscale[:, 0:1]).then_inc(tern0, 1)

            dve.wait_ge(blk_zero, 2)
            dve.wait_ge(pm_full, 1)
            ps = bank[6][:, 0:4 * H].rearrange("p (w j c s) -> p w s c j", w=2, j=2, s=2)
            bv = blk_v[:, :].rearrange("p (c n) -> p c n", n=68)
            for s in range(2):
                rows = slice(DH * s, DH * s + DH)
                dve.tensor_copy(blk_k[rows, :, s, :], ps[rows, 0, s, :, :])
                ins = dve.tensor_copy(bv[rows, :, 2 * s:2 * s + 2], ps[rows, 1, s, :, :])
            ins.then_inc(blk_done, 1)

            for b in range(B):
                dve.wait_ge(full_done, b + 1)
                full = yT_full[:, b, :].rearrange("p (k t) -> p k t", k=KC)
                at = slice(SEQ * b, SEQ * b + SEQ)
                link(dve.tensor_copy(xT[0][:, :, at], full))
                dve.tensor_tensor(xT[1][:, :, at], full, xT[0][:, :, at].bitcast(F32), ALU.subtract).then_inc(lo0_done, 1)

            for j in range(HC // 2):
                ps = unit("wq0T", j)
                if j >= 4:
                    dve.wait_ge(g_mm, j - 3)
                dve.tensor_copy(wq0T[:, j % 4, :], ps[:, :]).then_inc(rel["dve"], 1)
            dve.wait_ge(g_mm, HC // 2)
            dve.tensor_copy(g0[:, :, :], bank[6][:, 0:2 * P].rearrange("p (k n) -> p k n", k=KC)[:, :, 0:2 * H]).then_inc(g_done, 1)

            dve.wait_ge(ld["fc"], 16)
            dve.wait_ge(ld["proj"], 16)
            magnitude(1, nat_fc[:, :, :])
            magnitude(2, nat_proj[:, :, :]).then_inc(sum1_in, 1)
            dve.wait_ge(sum1_out, 1)
            link(dve.tensor_scalar(wscale[:, 1:3], bank[7][:, 0:2], 1.0 / (DIM * FF), None, ALU.mult))
            link(dve.tensor_scalar(wsum[:, 0:2], wscale[:, 1:3], EPS_BIT, None, ALU.add))
            link(dve.reciprocal(wsum[:, 0:2], wsum[:, 0:2]))
            ternary(nat_fc[:, :, :], wsum[:, 0:1])
            ternary(nat_proj[:, :, :], wsum[:, 1:2]).then_inc(tern1, 1)
            dve.wait_ge(m_full, 1)
            dve.tensor_copy(m0[:, :], bank[7][0:2 * H, 0:DIM]).then_inc(m_done, 1)

            ps = unit("score0")
            for b in range(B):
                at = slice(2 * H * b, 2 * H * b + 2 * H)
                ins = dve.tensor_scalar(small[:, 3, at], ps[:, at], f1[:, 2 * b + 1:2 * b + 2], None, ALU.mult)
            ins.then_inc(rel["dve"], 1)
            dve.wait_ge(rel["dve"], released("dve", UNIT[("score0", 0)]))
            pair = small[:, :, :].rearrange("p w (n j) -> p w n j", j=2)
            top = small[:, 2, 0:H * B]
            link(dve.tensor_tensor(top, pair[:, 3, :, 0], pair[:, 3, :, 1], ALU.max))
            for j in range(2):
                ins = dve.tensor_tensor(pair[:, 0, :, j], pair[:, 3, :, j], top, ALU.subtract)
            ins.then_inc(e_in, 1)
            dve.wait_ge(e_out, 1)
            link(dve.tensor_tensor(top, pair[:, 1, :, 0], pair[:, 1, :, 1], ALU.add))
            link(dve.reciprocal(top, top))
            for j in range(2):
                ins = dve.tensor_tensor(pair[:, 3, :, j], pair[:, 1, :, j], top, ALU.mult)
            ins.then_inc(prob0, 1)

            for j in range(QKV1 // 256):
                ps = unit("qkvT", j)
                at = slice(256 * j, 256 * j + 256)
                dve.wait_ge(hi_done, j + 1)
                dve.tensor_tensor(qkvT[1][:, :, at], ps[:, :].rearrange("p (k n) -> p k n", k=KC),
                                  qkvT[0][:, :, at].bitcast(F32), ALU.subtract).then_inc(rel["dve"], 1)

            for b in range(B):
                ps = unit("out0", b)
                ins = dve.tensor_tensor(x[:, b, :, :], x[:, b, :, :], ps[:, :].rearrange("p (e n) -> p e n", e=2), ALU.add)
                ins.then_inc(rel["dve"], 1)
            dve.wait_ge(rel["dve"], released("dve", UNIT[("out0", B - 1)]))
            layer_stats()
            rsqrt(r, var, EPS_LN)
            for t in range(8):
                ins = dve.tensor_scalar(y1[:, t // 2, t % 2, :], x[:, t // 2, t % 2, :], mean[:, t:t + 1], r[:, t:t + 1],
                                        ALU.subtract, ALU.mult)
                if t % 2:
                    ins.then_inc(y1_done, 1)
            link(dve.tensor_tensor(ms, r, r, ALU.mult))
            link(dve.tensor_tensor(ms, ms, var, ALU.mult))
            rsqrt(c2, ms, EPS_BIT)
            link(dve.reciprocal(f1, ms))
            link(dve.tensor_tensor(f1, f1, ms, ALU.mult))
            link(dve.tensor_tensor(c2, c2, f1, ALU.mult))
            for b in range(B):
                ps = unit("yT1", b)[:, :].rearrange("p (k e t) -> p k t e", k=KC, e=2)
                dve.wait_ge(hi_done, QKV1 // 256 + b + 1)
                for k in range(KC):
                    at = slice(SEQ * b, SEQ * b + SEQ)
                    ins = dve.tensor_tensor(xT[1][:, k, at].rearrange("p (t e) -> p t e", e=2), ps[:, k, :, :],
                                            xT[0][:, k, at].bitcast(F32).rearrange("p (t e) -> p t e", e=2), ALU.subtract)
                ins.then_inc(rel["dve"], 1)
            dve.tensor_scalar(ffac[:, :, 0], c2, wscale[:, 1:2], None, ALU.mult).then_inc(f_fac, 1)

            def hidden_lo(t):
                for half in range(2):
                    dve.wait_ge(f_hi, 2 * t + half + 1)
                    dve.tensor_tensor(hT[1][:, 4 * half:4 * half + 4, :], bank[4 + half][:, :].rearrange("p (k n) -> p k n", k=4),
                                      hT[0][:, 4 * half:4 * half + 4, :].bitcast(F32), ALU.subtract).then_inc(f_lo, 1)

            def ffn_add(t):
                dve.wait_ge(f_out, t + 1)
                dve.tensor_tensor(x[:, t // 2, t % 2, :], x[:, t // 2, t % 2, :], bank[6 + t % 2][:, 0:DIM],
                                  ALU.add).then_inc(f_add, 1)

            for t in range(8):
                if t >= 1:
                    hidden_lo(t - 1)
                dve.wait_ge(f_gelu, t + 1)
                dve.bn_stats(fstat[:, t, 0:6], ffn_h[:, t % 2, 0:512])
                link(dve.bn_stats(fstat[:, t, 6:12], ffn_h[:, t % 2, 512:1024]))
                link(dve.bn_aggr(fmv[:, t, :], fstat[:, t, :]))
                fm, fv = fmv[:, t, 0:1], fmv[:, t, 1:2]
                rsqrt(ffac[:, t, 1:2], fv, EPS_BIT)
                link(dve.reciprocal(ffac[:, t, 2:3], fv))
                link(dve.tensor_tensor(ffac[:, t, 2:3], ffac[:, t, 2:3], fv, ALU.mult))
                link(dve.tensor_scalar(ffac[:, t, 3:4], ffac[:, t, 1:2], ffac[:, t, 2:3], wscale[:, 2:3], ALU.mult, ALU.mult))
                dve.tensor_scalar(ffn_h[:, t % 2, :], ffn_h[:, t % 2, :], fm, ffac[:, t, 3:4],
                                  ALU.subtract, ALU.mult).then_inc(f_y, 1)
                if t >= 1:
                    ffn_add(t - 1)
            hidden_lo(7)
            ffn_add(7)

            def rope_q(c, it):
                ps, full, free, n = place(f"q{c}", it)
                dve.wait_ge(full, n + 1)
                if it is not -1:
                    dve.wait_ge(qn_done, it * 2 + c + 1)
                q = ps[:, :].rearrange("p (h s d) -> p h s d", h=HG, s=2)
                cos = cst[:, C_QC + DH * c:C_QC + DH * c + DH].rearrange("p (a n) -> p a n", a=1).to_broadcast([P, HG, DH])
                sin = cst[:, C_QS + DH * c:C_QS + DH * c + DH].rearrange("p (a s d) -> p a s d", a=1, s=2)
                dve.tensor_tensor(rope_a[:, c, :].rearrange("p (h d) -> p h d", h=HG), ps[:, :].rearrange("p (h d) -> p h d", h=HG),
                                  cos, ALU.mult)
                b4 = rope_b[:, c, :].rearrange("p (h s d) -> p h s d", h=HG, s=2)
                for s in range(2):
                    ins = dve.tensor_tensor(b4[:, :, s, :], q[:, :, 1 - s, :],
                                            sin[:, :, s, :].to_broadcast([P, HG, DH // 2]), ALU.mult)
                ins.then_inc(free, 1)

            def rope_kv(it):
                ps, full, free, n = place("kv", it)
                dve.wait_ge(full, n + 1)
                if it is not -1:
                    dve.wait_ge(kn_done, it + 1)
                kv = ps[:, 0:2 * P].rearrange("p (c w d) -> p c w d", c=2, w=2)
                cos = cst[:, C_KC:C_KC + P].rearrange("p (c d) -> p c d", c=2)
                sin = cst[:, C_KS:C_KS + P].rearrange("p (c s d) -> p c s d", c=2, s=2)
                dve.tensor_tensor(rope_k[:, 0, :, :], kv[:, :, 0, :], cos, ALU.mult)
                for s in range(2):
                    d = DH // 2
                    dve.tensor_tensor(rope_k[:, 1, :, d * s:d * s + d], kv[:, :, 0, d * (1 - s):d * (1 - s) + d],
                                            sin[:, :, s, :], ALU.mult)
                dve.tensor_copy(v_stage, kv[:, :, 1, :]).then_inc(free, 1)

            def maxima(it, u):
                n = it * UNITS + u
                dve.wait_ge(s_full, n + 1)
                heads = 4 if u < 2 else 2
                h = 4 * u if u < 2 else 8 + 2 * (u - 2)
                dve.tensor_reduce(neg_max[:, h:h + heads], bank[u % 2][:, :].rearrange("p (h k) -> p h k", h=heads),
                                  AX.X, ALU.max, negate=True).then_inc(s_max, 1)

            def normalise(it, c):
                dve.wait_ge(pv_done, it * UNITS + (2 if c == 0 else 6))
                dve.reciprocal(rsum[:, 8 * c:8 * c + 8], sums[:, 8 * c:8 * c + 8]).then_inc(rs_done, 1)
                dve.wait_ge(rs_done, it * 2 + c + 1)
                dve.tensor_tensor(o_n[:, c, :].rearrange("p (h d) -> p h d", h=HG),
                                  bank[4 + c][:, :].rearrange("p (h d) -> p h d", h=HG),
                                  rsum[:, 8 * c:8 * c + 8].rearrange("p (h a) -> p h a", a=1).to_broadcast([P, HG, DH]),
                                  ALU.mult).then_inc(normed, 1)

            def values():
                dve.tensor_copy(v, v_stage).then_inc(v_done, 1)

            def add_out(it, e, last=False):
                ps, full, free, n = place(f"wo{e}", it, last)
                dve.wait_ge(full, n + 1)
                b = (it - 1) // HKV
                if isinstance(b, int):
                    dst = x[:, b:b + 1, e, :]
                else:
                    dst = x[:, bass.ds(b, 1), e, :]
                dve.tensor_tensor(dst, dst, ps[:, 0:DIM].rearrange("p (a n) -> p a n", a=1), ALU.add).then_inc(free, 1)

            def iteration(it, first=False, last=False):
                maxima(it, 0)
                maxima(it, 1)
                if not last:
                    rope_q(0, it)
                maxima(it, 2)
                if not last:
                    rope_q(1, it)
                maxima(it, 3)
                if not first:
                    add_out(it, 0)
                maxima(it, 4)
                if not first:
                    add_out(it, 1)
                if not last:
                    rope_kv(it)
                normalise(it, 0)
                maxima(it, 5)
                normalise(it, 1)
                if not last:
                    values()

            rope_q(0, -1)
            rope_q(1, -1)
            rope_kv(-1)
            dve.wait_ge(free7, 3)
            values()
            iteration(0, first=True)
            with dve.Fori(1, ITS - 1) as it:
                iteration(it)
            iteration(ITS - 1, last=True)
            for e in range(2):
                add_out(ITS, e, last=True)

        @block.tensor
        def _(pe):
            def ring(what, j=0):
                n = UNIT[(what, j)]
                if n >= RING:
                    engine = RELEASES[ORDER[n - RING][0]]
                    pe.wait_ge(rel[engine], released(engine, n - RING))
                return bank[n % RING]

            def transposes(ps, blocks):
                for j, a in enumerate(blocks):
                    ins = pe.transpose(ps[:, P * j:P * j + P], a, ident)
                return ins

            pe.wait_ge(ld["cst"], 16)
            ones = cst[:, C_ONE:C_ONE + P]
            pe.wait_ge(sum0_in, 1)
            pe.matmul(bank[7][:, 0:1], ones, wsum[:, 0:1], start=True, stop=True).then_inc(sum0_out, 1)
            pe.wait_ge(ld["pm"], 64)
            for w in range(2):
                for j in range(2):
                    at = (2 * w + j) * H
                    ins = pe.transpose(bank[6][:, at:at + H], pmn[:, w, j, :, :].rearrange("p a d -> p (a d)"), cst[0:H, C_ID:C_ID + H])
            ins.then_inc(pm_full, 1)
            for b in range(B):
                ps = ring("yT0", b)
                pe.wait_ge(y_done, b + 1)
                transposes(ps, [y0[:, b, e, P * k:P * k + P] for k in range(KC) for e in range(2)]).then_inc(filled, 1)
            ps = ring("ffn0T")
            pe.wait_ge(tern0, 1)
            transposes(ps, [nat_ffn0[:, o, P * k:P * k + P] for k in range(KC) for o in range(2)]).then_inc(filled, 1)

            wq = wq0[:, :].rearrange("p (k n) -> p k n", k=KC)

            def g_products(j):
                pe.wait_ge(rel["dve"], released("dve", UNIT[("wq0T", j)]))
                for i in range(2):
                    c = 2 * j + i
                    for k in range(KC):
                        at = P * k + 4 * c
                        ins = pe.matmul(bank[6][:, at:at + 4], wq0T[:, j % 4, 256 * i + P * k:256 * i + P * k + P],
                                        blk_k[:, c, :, :].rearrange("p s j -> p (s j)"), start=True, stop=True)
                ins.then_inc(g_mm, 1)
                return ins

            pe.wait_ge(ld["wq0"], 16)
            for j in range(HC // 2):
                ps = ring("wq0T", j)
                transposes(ps, [wq[:, k, P * c:P * c + P] for c in (2 * j, 2 * j + 1) for k in range(KC)]).then_inc(filled, 1)
                if j == 1:
                    pe.wait_ge(blk_done, 1)
                if j >= 1:
                    g_products(j - 1)
            g_products(HC // 2 - 1)

            pe.wait_ge(sum1_in, 1)
            pe.matmul(bank[7][:, 0:2], ones, wsum[:, 1:3], start=True, stop=True).then_inc(sum1_out, 1)
            pe.wait_ge(ld["wout"], 16)
            pe.wait_ge(tern1, 1)
            for c in range(HC):
                ins = pe.matmul(bank[7][0:2 * H, 0:DIM], blk_v[:, 64 * c:64 * c + 64], wo_t[:, c, :],
                                start=c == 0, stop=c == HC - 1)
            ins.then_inc(m_full, 1)

            ps = ring("score0")
            pe.wait_ge(g_done, 1)
            pe.wait_ge(rel["act"], released("act", UNIT[("yT0", B - 1)]))
            for b in range(B):
                for k in range(KC):
                    ins = pe.matmul(ps[:, 2 * H * b:2 * H * b + 2 * H], xrT[:, k, P * b:P * b + P], g0[:, k, :],
                                    start=k == 0, stop=k == KC - 1)
            ins.then_inc(filled, 1)

            pe.wait_ge(ld["qkv"], 16)
            for j in range(QKV1 // 256):
                ps = ring("qkvT", j)
                transposes(ps, [nat_qkv[:, c, P * k:P * k + P] for k in range(KC) for c in (2 * j, 2 * j + 1)]).then_inc(filled, 1)

            ps = ring("probT0")
            pe.wait_ge(prob0, 1)
            for b in range(B):
                ins = pe.transpose(ps[0:2 * H, P * b:P * b + P], small[:, 3, 2 * H * b:2 * H * b + 2 * H], ident)
            ins.then_inc(filled, 1)

            pe.wait_ge(m_done, 1)
            pe.wait_ge(lo0_done, B)
            pe.wait_ge(ld["vec"], 32)
            for b in range(B):
                ps = ring("out0", b)
                if b == 0:
                    pe.wait_ge(rel["act"], released("act", UNIT[("probT0", 0)]))
                for e in range(2):
                    o = ps[:, DIM * e:DIM * e + DIM]
                    pe.matmul(o, ones[0:1, :], bias_row[:, :], start=True, stop=False)
                    p = probT0[:, P * b:P * b + P] if e else cst[0:2 * H, C_EVEN:C_EVEN + P]
                    pe.matmul(o, p, m0[:, :], start=False, stop=False)
                    for k in range(KC):
                        for s in range(2):
                            at = SEQ * b + P * e
                            ins = pe.matmul(o, xT[s][:, k, at:at + P], ffn0T[:, k, :], start=False,
                                            stop=k == KC - 1 and s == 1)
                ins.then_inc(filled, 1)

            pe.wait_ge(ld["o"], 16)
            for j in range(HC // 2):
                ps = ring("woT", j)
                transposes(ps, [nat_o[:, k, P * c:P * c + P] for c in (2 * j, 2 * j + 1) for k in range(2)]).then_inc(filled, 1)
            for j in range(FF // 256):
                ps = ring("fcT", j)
                transposes(ps, [nat_fc[:, c, P * k:P * k + P] for k in range(KC) for c in (2 * j, 2 * j + 1)]).then_inc(filled, 1)
            for j in range(FF // 256):
                ps = ring("projT", j)
                transposes(ps, [nat_proj[:, k, P * c:P * c + P] for c in (2 * j, 2 * j + 1) for k in range(2)]).then_inc(filled, 1)
            for b in range(B):
                ps = ring("yT1", b)
                pe.wait_ge(y1_done, b + 1)
                transposes(ps, [y1[:, b, e, P * k:P * k + P] for k in range(KC) for e in range(2)]).then_inc(filled, 1)

            def fc(t):
                if t >= 2:
                    pe.wait_ge(f_gelu, t - 1)
                at = SEQ * (t // 2) + t % 2
                for half in range(2):
                    n = 0
                    for k in range(KC):
                        for s in range(2):
                            ins = pe.matmul(bank[2 * (t % 2) + half][:, :], xT[s][:, k, at:at + 2 * P - 1:2],
                                            fcT[:, k, 512 * half:512 * half + 512], start=n == 0, stop=n == 3)
                            n += 1
                ins.then_inc(f_fc, 1)

            def hidden_T(t):
                pe.wait_ge(f_y, t + 1)
                if t >= 1:
                    pe.wait_ge(f_lo, 2 * t)
                for half in range(2):
                    transposes(bank[4 + half], [ffn_h[:, t % 2, P * k:P * k + P] for k in range(4 * half, 4 * half + 4)]
                               ).then_inc(f_T, 1)

            def proj(t):
                pe.wait_ge(f_lo, 2 * t + 2)
                if t >= 2:
                    pe.wait_ge(f_add, t - 1)
                n = 0
                for k in range(FF // P):
                    for s in range(2):
                        ins = pe.matmul(bank[6 + t % 2][:, 0:DIM], hT[s][:, k, :], projT[:, k, :], start=n == 0, stop=n == 2 * FF // P - 1)
                        n += 1
                ins.then_inc(f_out, 1)

            pe.wait_ge(rel["act"], released("act", len(ORDER) - 1))
            pe.wait_ge(rel["dve"], released("dve", len(ORDER) - 1))
            fc(0)
            fc(1)
            for t in range(8):
                hidden_T(t)
                if t + 2 < 8:
                    fc(t + 2)
                proj(t)
            pe.wait_ge(f_add, 8)

            W = [(0, 0), (1, 0), (0, 1)]

            def group_cols(w, k, it, what):
                g = (it + 1) % HKV
                if what == "q":
                    return w[:, k, bass.ds(g * (HG * DH), HG * DH)]
                kv = w[:, k, H * DH:QKV1].rearrange("p (w n) -> p w n", w=2)
                return kv[:, :, bass.ds(g * DH, DH)]

            def project_q(c, it):
                ps, full, free, n = place(f"q{c}", it)
                pe.wait_ge(free, n)
                if c == 0:
                    pe.wait_ge(xb_done, it + 2)
                i = 0
                for s, w in W:
                    for k in range(KC):
                        ins = pe.matmul(ps[:, :], xb[s][:, 2 * k + c, :], group_cols(qkvT[w], k, it, "q"), start=i == 0, stop=i == 5)
                        i += 1
                ins.then_inc(full, 1)

            def project_kv(it):
                ps, full, free, n = place("kv", it)
                pe.wait_ge(free, n)
                for c in range(2):
                    i = 0
                    for s, w in W:
                        for k in range(KC):
                            ins = pe.matmul(ps[:, P * c:P * c + P].rearrange("p (w d) -> p w d", w=2), xb[s][:, 2 * k + c, :],
                                            group_cols(qkvT[w], k, it, "kv"), start=i == 0, stop=i == 5)
                            i += 1
                ins.then_inc(full, 1)

            def turn(what, it):
                ps, full, free, n = place(what, it)
                pe.wait_ge(free, n)
                if what == "kT":
                    pe.wait_ge(kn_done, it + 2)
                    blocks = [k_nat[:, s, c, :, :].rearrange("p w d -> p (w d)") for s in range(2) for c in range(2)]
                else:
                    j = int(what[2])
                    c, h = j // 2, 4 * (j % 2)
                    pe.wait_ge(qn_done, it * 2 + 2 + c + 1)
                    blocks = [q_nat[:, c, h + i, :, :].rearrange("p s d -> p (s d)") for i in range(4)]
                transposes(ps, blocks).then_inc(full, 1)

            def scores(it, u, first=False):
                n = it * UNITS + u
                if u == 0:
                    pe.wait_ge(free7, it * 6 + 6)
                    pe.wait_ge(free6, 2 if first else it * 6 - 2)
                if u >= 2 or not first:
                    pe.wait_ge(s_exp, n - 1)
                ps = bank[u % 2]
                heads, c = (4, 0) if u < 2 else (2, 1)
                keys = P * (c + 1)
                h = 4 * u if u < 2 else 2 * (u - 2)
                for j in range(heads):
                    for s in range(2):
                        pe.matmul(ps[:, keys * j:keys * j + keys], qT[:, h + j, P * c:P * c + P], kT[:, s, 0:keys],
                                  start=j == 0 and s == 0, stop=False, skip_group_check=True)
                diag = ps[:, :].rearrange("p (h k) -> p h k", h=heads)[:, :, P * c:P * c + P]
                pe.matmul(diag, ident_b[:, :], mask_b[:, 0:heads, :], start=False, stop=True,
                          skip_group_check=True).then_inc(s_full, 1)

            def prob_T(it, u, first=False):
                n = it * UNITS + u
                pe.wait_ge(s_exp, n + 1)
                if u >= 2 or not first:
                    pe.wait_ge(t_done, n - 1)
                transposes(bank[2 + u % 2], [prob[u % 3][:, P * j:P * j + P] for j in range(4)]).then_inc(t_full, 1)

            def heads_out(it, u, first=False):
                n = it * UNITS + u
                pe.wait_ge(t_done, n + 1)
                if u == 0:
                    pe.wait_ge(v_done, it + 1)
                if u in (0, 2) and not first:
                    pe.wait_ge(normed, it * 2 - (1 if u == 0 else 0))
                for j in range(4 if u < 2 else 2):
                    if u < 2:
                        at = DH * (4 * u + j)
                        ins = pe.matmul(bank[4][:, at:at + DH], probT[u % 3][:, P * j:P * j + P], v[:, 0, :], start=True, stop=True)
                    else:
                        at = DH * (2 * (u - 2) + j)
                        for k in range(2):
                            ins = pe.matmul(bank[5][:, at:at + DH], probT[u % 3][:, P * (2 * j + k):P * (2 * j + k) + P], v[:, k, :],
                                            start=k == 0, stop=k == 1)
                ins.then_inc(pv_done, 1)

            def turn_heads(c, it, last=False):
                ps, full, free, n = place(f"oT{c}", it, last)
                pe.wait_ge(free, n)
                pe.wait_ge(normed, it * 2 - 1 + c)
                transposes(ps, [o_n[:, c, P * j:P * j + P] for j in range(4)]).then_inc(full, 1)

            def project_out(e, it, last=False):
                ps, full, free, n = place(f"wo{e}", it, last)
                pe.wait_ge(free, n)
                g = (it - 1) % HKV
                for j in range(4):
                    rhs = wo_t[:, bass.ds(g * 4 + j, 1), :].rearrange("p a n -> p (a n)")
                    ins = pe.matmul(ps[:, 0:DIM], oT[:, j, e:e + 2 * P - 1:2], rhs, start=j == 0, stop=j == 3)
                ins.then_inc(full, 1)

            def iteration(it, first=False, last=False):
                scores(it, 0, first)
                if not first:
                    turn_heads(0, it)
                scores(it, 1, first)
                if not last:
                    project_q(0, it)
                if not first:
                    turn_heads(1, it)
                scores(it, 2, first)
                prob_T(it, 0, first)
                if not last:
                    project_q(1, it)
                scores(it, 3, first)
                prob_T(it, 1, first)
                heads_out(it, 0, first)
                if not first:
                    project_out(0, it)
                scores(it, 4, first)
                prob_T(it, 2, first)
                heads_out(it, 1, first)
                if not first:
                    project_out(1, it)
                if not last:
                    project_kv(it)
                scores(it, 5, first)
                prob_T(it, 3, first)
                heads_out(it, 2, first)
                prob_T(it, 4, first)
                heads_out(it, 3, first)
                if not last:
                    turn("qT0", it)
                    turn("qT1", it)
                prob_T(it, 5, first)
                heads_out(it, 4, first)
                if not last:
                    turn("qT2", it)
                    turn("qT3", it)
                    turn("kT", it)
                heads_out(it, 5, first)

            project_q(0, -1)
            project_q(1, -1)
            project_kv(-1)
            for what in ("qT0", "qT1", "qT2", "qT3", "kT"):
                turn(what, -1)
            pe.wait_ge(const_done, 1)
            iteration(0, first=True)
            with pe.Fori(1, ITS - 1) as it:
                iteration(it)
            iteration(ITS - 1, last=True)
            for c in range(2):
                turn_heads(c, ITS, last=True)
            for e in range(2):
                project_out(e, ITS, last=True)


_INS = ["L0_attn_seq", "L0_attn_w_qkv", "L0_attn_w_out", "L0_attn_pm", "L0_ffn_weight", "L0_ffn_bias",
        "L1_attn_w_qkv", "L1_attn_w_o", "L1_ffn_w_fc", "L1_ffn_w_proj"]
_VECS = ["L0_ffn_ln_gamma", "L0_ffn_ln_beta", "L0_attn_w_norm"]


def kernel(**inputs):
    import concourse.bacc as bacc
    from concourse.bass_utils import run_bass_kernel_spmd

    nc = bacc.Bacc("TRN2", target_bir_lowering=False, num_devices=1)
    arrays, args = {}, []
    for name in _INS:
        a = np.ascontiguousarray(inputs[name])
        arrays[f"in_{name}_dram"] = a
        args.append(nc.dram_tensor(f"in_{name}_dram", a.shape, mybir.dt.from_np(a.dtype), kind="ExternalInput").ap())
    arrays["vec_dram"] = np.ascontiguousarray(np.stack([np.asarray(inputs[n]).reshape(KC, P) for n in _VECS]).transpose(2, 0, 1))
    args.append(nc.dram_tensor("vec_dram", (P, len(_VECS), KC), F32, kind="ExternalInput").ap())
    arrays["const_dram"] = constants()
    args.append(nc.dram_tensor("const_dram", (P, C_ALL), F32, kind="ExternalInput").ap())
    args.append(nc.dram_tensor("out_0_dram", (B, SEQ, DIM), F32, kind="ExternalOutput").ap())
    build(nc, *args)
    r = run_bass_kernel_spmd(nc, [arrays], core_ids=[0])
    return r.results[0]["out_0_dram"]
```

```python
from contextlib import ExitStack

import numpy as np

import concourse.bass as bass
from concourse import mybir

F32 = mybir.dt.float32
F32R = mybir.dt.float32r
BF16 = mybir.dt.bfloat16
ALU = mybir.AluOpType
ACT = mybir.ActivationFunctionType
AX = mybir.AxisListType

P = 128
B, SEQ, DIM = 4, 256, 256
KC = DIM // P
H, DH = 32, 64
HKV = 4
HG = H // HKV
HC = H * DH // P
QKV1 = (H + 2 * HKV) * DH
FF = 4 * DIM
THETA = 10000.0
EPS_LN, EPS_BIT = 1e-5, 1e-6
EPS_RMS = float(np.finfo(np.float32).eps)
MAGIC = 1.5 * 2.0 ** 23
MASKED = -1e30
RING = 6
ITS = B * HKV
UNITS = 6

C_ID, C_MASK, C_EVEN, C_ONE, C_QC, C_QS, C_KC, C_KS = (P * i for i in range(8))
C_ALL = 8 * P


def constants():
    c = np.zeros((P, C_ALL), np.float32)
    c[:, C_ID:C_ID + P] = np.eye(P)
    c[:, C_MASK:C_MASK + P] = np.where(np.arange(P)[None] > np.arange(P)[:, None], MASKED, 0.0)
    c[0:2 * H:2, C_EVEN:C_EVEN + P] = 1.0
    c[2 * H, C_EVEN:C_EVEN + P] = 1.0
    c[:, C_ONE:C_ONE + P] = 1.0
    inv = (1.0 / np.float32(THETA) ** (np.arange(0, DH, 2, dtype=np.float32) / np.float32(DH))).astype(np.float32)
    for t in range(2):
        ang = (np.arange(P, dtype=np.float32) + np.float32(P * t))[:, None] * inv[None]
        cos = np.cos(ang).astype(np.float32)
        sin = np.sin(ang).astype(np.float32)
        cc, ss = np.concatenate([cos, cos], 1), np.concatenate([-sin, sin], 1)
        at = DH * t
        c[:, C_QC + at:C_QC + at + DH] = cc * np.float32(DH ** -0.5)
        c[:, C_QS + at:C_QS + at + DH] = ss * np.float32(DH ** -0.5)
        c[:, C_KC + at:C_KC + at + DH] = cc
        c[:, C_KS + at:C_KS + at + DH] = ss
    return c


ORDER = ([("wq0T", j) for j in range(HC // 2)] + [("yT0", b) for b in range(B)] + [("ffn0T", 0), ("score0", 0)]
         + [("qkvT", j) for j in range(5)] + [("probT0", 0)] + [("out0", b) for b in range(B)]
         + [("qkvT", j) for j in range(5, QKV1 // 256)] + [("fcT", j) for j in range(FF // 256)]
         + [("projT", j) for j in range(FF // 256)] + [("yT1", b) for b in range(B)])
UNIT = {key: n for n, key in enumerate(ORDER)}
RELEASES = {"yT0": "act", "ffn0T": "act", "wq0T": "act", "score0": "dve", "qkvT": "dve", "probT0": "act",
            "out0": "dve", "fcT": "act", "projT": "act", "yT1": "dve"}


def released(engine, n):
    return sum(RELEASES[what] == engine for what, _ in ORDER[:n + 1])


def build(nc, seq, w_qkv0, w_out0, pm, w_ffn0, bias0, w_qkv1, w_o1, w_fc, w_proj, vec, const, out):
    with ExitStack() as ctx:
        def sb(name, shape, dt=F32):
            return ctx.enter_context(nc.sbuf_tensor(name, shape, dt))

        def sem(name):
            return ctx.enter_context(nc.semaphore(name))

        bank = [ctx.enter_context(nc.psum_tensor(f"bank{i}", [P, 512], F32)) for i in range(8)]

        cst = sb("cst", [P, C_ALL])
        ident = cst[:, C_ID:C_ID + P]
        ident_b = sb("ident_b", [P, P], BF16)
        mask_b = sb("mask_b", [P, 4, P], BF16)
        x = sb("x", [P, B, 2, DIM])
        stats = sb("stats", [P, 8, 6])
        mv = sb("mv", [P, 8, 2])
        tok = sb("tok", [P, 8, 8])
        fstat = sb("fstat", [P, 8, 12])
        fmv = sb("fmv", [P, 8, 2])
        ffac = sb("ffac", [P, 8, 8])
        vecs = sb("vecs", [P, 3, KC])
        neg_half = sb("neg_half", [P, 8])
        wsum = sb("wsum", [P, 4])
        wscale = sb("wscale", [P, 4])
        winv = sb("winv", [P, 4])
        blk_k = sb("blk_k", [P, HC, 2, 2])
        neg_max = [sb(f"neg_max{i}", [P, 16]) for i in range(2)]
        sums = [sb(f"sums{i}", [P, 16]) for i in range(2)]
        rsum = [sb(f"rsum{i}", [P, 16]) for i in range(2)]

        base = (nc.sbuf_base + 63) // 64 * 64
        ends = [0]

        def at(name, offset, shape, dt=F32):
            ends[0] = max(ends[0], offset + 4 * int(np.prod(shape[1:])))
            return nc.alloc_sbuf_tensor_at(name, shape, dt, offset=base + offset)

        K = 1024
        qkvT = [at(f"qkvT_{w}", 20 * K * i, [P, KC, QKV1], F32R) for i, w in enumerate(("hi", "lo"))]
        xT = [at(f"xT_{w}", 40 * K + 8 * K * i, [P, KC, B * SEQ], F32R) for i, w in enumerate(("hi", "lo"))]
        fcT = at("fcT", 56 * K, [P, KC, FF], F32R)
        projT = at("projT", 64 * K, [P, FF // P, DIM], F32R)
        woT = [at(f"woT_{w}", 72 * K + 16 * K * i, [P, HC, DIM], F32R) for i, w in enumerate(("hi", "lo"))]
        blk_v = at("blk_v", 72 * K, [P, HC * 68])
        small = at("small", 77 * K, [P, 4, 2 * H * B])
        probT0 = at("probT0", 81 * K, [2 * H + 1, B * P])
        xrT = at("xrT", 83 * K, [P, KC, B * P])
        wout0 = at("wout0", 88 * K, [P, HC, DIM])
        wq0 = at("wq0", 104 * K, [P, KC, H * DH])
        y1 = at("y1", 104 * K, [P, B, 2, DIM])
        ffn_h = at("ffn_h", 112 * K, [P, 2, FF])
        kT = [at(f"kT{i}", 104 * K + 2 * K * i, [P, 2, SEQ], F32R) for i in range(2)]
        k_nat = at("k_nat", 108 * K, [P, 2, 2, 2, DH])
        rope_k = at("rope_k", 110 * K, [P, 2, 2, DH])
        v = [at(f"v{i}", 111 * K + K // 2 * i, [P, 2, DH]) for i in range(2)]
        oT = [at(f"oT_{w}", 112 * K + 4 * K * i, [P, 4, SEQ], F32R) for i, w in enumerate(("hi", "lo"))]
        nat_qkv = at("nat_qkv", 120 * K, [P, QKV1 // P, DIM])
        qT = [at(f"qT{i}", 120 * K + 8 * K * i, [P, HG, SEQ], F32R) for i in range(2)]
        xb = [at(f"xb_{w}", 136 * K + 2 * K * i, [P, 4, P], F32R) for i, w in enumerate(("hi", "lo"))]
        hT = [[at(f"hT{i}_{w}", 140 * K + 8 * K * i + 4 * K * j, [P, FF // P, P], F32R) for j, w in enumerate(("hi", "lo"))]
              for i in range(2)]
        prob = [at(f"prob{i}", 140 * K + 2 * K * i, [P, 512]) for i in range(3)]
        probT = [at(f"probT{i}", 146 * K + 2 * K * i, [P, 512]) for i in range(3)]
        o_n = at("o_n", 152 * K, [P, 2, 512])
        yT_full = at("yT_full", 156 * K, [P, B, 512])
        nat_fc = at("nat_fc", 156 * K, [P, FF // P, DIM])
        q_nat = at("q_nat", 156 * K, [P, 2, HG, 2, DH])
        y0 = at("y0", 164 * K, [P, B, 2, DIM])
        nat_proj = at("nat_proj", 164 * K, [P, 2, FF])
        rope_a = at("rope_a", 164 * K, [P, 2, 512])
        rope_b = at("rope_b", 168 * K, [P, 2, 512])
        nat_o = at("nat_o", 172 * K, [P, 2, H * DH])
        nat_ffn0 = at("nat_ffn0", 172 * K, [P, 2, DIM])
        ffn0T = at("ffn0T", 174 * K, [P, KC, DIM], F32R)
        pmn = at("pmn", 176 * K, [H, 2, 2, 2, DH])
        wq0T = at("wq0T", 140 * K, [P, 4, 512])
        m0 = at("m0", 148 * K, [2 * H + 1, DIM])
        g0 = at("g0", 150 * K, [P, KC, 2 * H])
        assert base + ends[0] <= nc.sbuf_usable_end

        ld = {n: sem("ld_" + n) for n in ("x", "cst", "vec", "bias", "pm", "ffn0", "wq0", "wout", "qkv", "o", "fc", "proj")}
        s_dve, s_pool = sem("s_dve"), sem("s_pool")
        filled = sem("filled")
        rel = {"act": sem("rel_act"), "dve": sem("rel_dve")}
        hi_done = sem("hi_done")
        root_in, root_out = sem("root_in"), sem("root_out")
        const_done = sem("const_done")
        y0_done, y1_done = sem("y0_done"), sem("y1_done")
        sum0_in, sum0_out = sem("sum0_in"), sem("sum0_out")
        sum1_in, sum1_out, inv1 = sem("sum1_in"), sem("sum1_out"), sem("inv1")
        tern0, tern_fc, tern_proj = sem("tern0"), sem("tern_fc"), sem("tern_proj")
        lo0_done = sem("lo0_done")
        zeroed, pm_full, blk_done = sem("zeroed"), sem("pm_full"), sem("blk_done")
        g_mm, g_done, m_full, m_done = sem("g_mm"), sem("g_done"), sem("m_full"), sem("m_done")
        e_in, e_out, prob0 = sem("e_in"), sem("e_out"), sem("prob0")
        f_fac, f_fc, f_gelu, f_norm, f_y, f_T, f_hi, f_lo, f_out, f_add = (
            sem("f_" + n) for n in ("fac", "fc", "gelu", "norm", "y", "T", "hi", "lo", "out", "add"))
        wo_full, wo_hi, wo_lo = sem("wo_full"), sem("wo_hi"), sem("wo_lo")
        xb_done = sem("xb_done")
        full = {6: sem("full6"), 7: sem("full7")}
        free = {6: sem("free6"), 7: sem("free7")}
        qn_done, kn_done = sem("qn_done"), sem("kn_done")
        s_full, s_max, s_exp, t_full, t_done, pv_done = (sem(n) for n in
                                                         ("s_full", "s_max", "s_exp", "t_full", "t_done", "pv_done"))
        rs_done, normed, oT_hi = sem("rs_done"), sem("normed"), sem("oT_hi")
        stored = sem("stored")
        block = ctx.enter_context(nc.Block())

        FILLS = {7: ["q0", "oT0", "qT0", "qT2", "qT3", "wo0"], 6: ["q1", "kv", "qT1", "oT1", "kT", "wo1"]}
        BEFORE, FIRST, INNER, LAST, AFTER = range(5)

        def place(what, it, kind):
            b = 7 if what in FILLS[7] else 6
            there = [w for w in FILLS[b] if (w[0:2] in ("oT", "wo") and kind in (INNER, LAST, AFTER))
                     or (w[0] in "qk" and kind in (BEFORE, FIRST, INNER))]
            before = {BEFORE: 0, FIRST: 4, LAST: (ITS - 1) * 6 + 2, AFTER: (ITS - 1) * 6 + 4}
            return b, (before[kind] if kind in before else it * 6 + 2) + there.index(what)

        def iterations(engine, iteration):
            iteration(0, 0, FIRST)
            with engine.Fori(1, ITS - 1, 2) as it:
                iteration(it, 1, INNER)
                iteration(it + 1, 0, INNER)
            iteration(ITS - 1, 1, LAST)

        def unit_heads(u):
            return (4, 4 * u, P) if u < 2 else (2, 2 * (u - 2), 2 * P)

        PROJ_BANK = [6, 6, 6, 6, 6, 0, 1, 0]

        @block.sync
        def _(sp):
            sp.dma_start(x[:, :, :, :], seq.rearrange("b (p e) d -> p b e d", e=2)).then_inc(ld["x"], 16)
            sp.dma_start(cst[:, :], const).then_inc(ld["cst"], 16)
            for w in range(2):
                for d in range(2):
                    sp.dma_start(pmn[:, w, :, d, :], pm[w, :, 0:2, :]).then_inc(ld["pm"], 16)
            sp.dma_start(wq0[:, :, :], w_qkv0.rearrange("(c p) n -> p c n", p=P)[:, :, 0:H * DH]).then_inc(ld["wq0"], 16)
            sp.dma_start(nat_ffn0[:, :, :], w_ffn0.rearrange("(c p) i -> p c i", p=P)).then_inc(ld["ffn0"], 16)
            sp.dma_start(wout0[:, :, :], w_out0.rearrange("(c p) n -> p c n", p=P)).then_inc(ld["wout"], 16)
            sp.dma_start(nat_qkv[:, :, :], w_qkv1.rearrange("(c p) n -> p c n", p=P)).then_inc(ld["qkv"], 16)
            sp.wait_ge(filled, UNIT[("yT0", B - 1)] + 1)
            sp.dma_start(nat_proj[:, :, :], w_proj.rearrange("(c p) n -> p c n", p=P)).then_inc(ld["proj"], 16)
            sp.wait_ge(lo0_done, B)
            sp.dma_start(nat_fc[:, :, :], w_fc.rearrange("(c p) n -> p c n", p=P)).then_inc(ld["fc"], 16)
            sp.wait_ge(filled, UNIT[("out0", B - 1)] + 1)
            sp.dma_start(nat_o[:, :, :], w_o1.rearrange("(c p) n -> p c n", p=P)).then_inc(ld["o"], 16)
            for b, w in ((7, "wo0"), (6, "wo1")):
                sp.wait_ge(free[b], place(w, ITS, AFTER)[1] + 1)
            sp.dma_start(out.rearrange("b (p e) d -> p b e d", e=2), x[:, :, :, :]).then_inc(stored, 16)
            sp.wait_ge(stored, 16)

        @block.scalar
        def _(act):
            act.dma_start(vecs[:, :, :], vec).then_inc(ld["vec"], 16)
            act.dma_start(m0[2 * H:2 * H + 1, :], bias0.rearrange("(a n) -> a n", a=1)).then_inc(ld["bias"], 16)

            def unit(what, j=0):
                n = UNIT[(what, j)]
                act.wait_ge(filled, n + 1)
                return bank[n % RING]

            act.wait_ge(zeroed, 3)
            act.wait_ge(pm_full, 1)
            ps = bank[6][:, 0:4 * H].rearrange("p (w j c s) -> p w s c j", w=2, j=2, s=2)
            bv = blk_v[:, :].rearrange("p (c n) -> p c n", n=68)
            for s in range(2):
                rows = slice(DH * s, DH * s + DH)
                nc.scalar.activation(blk_k[rows, :, s, :], ps[rows, 0, s, :, :], ACT.Copy)
                ins = nc.scalar.activation(bv[rows, :, 2 * s:2 * s + 2], ps[rows, 1, s, :, :], ACT.Copy)
            ins.then_inc(blk_done, 1)
            for j in range(HC // 2):
                ps = unit("wq0T", j)
                if j >= 4:
                    act.wait_ge(g_mm, j - 3)
                nc.scalar.activation(wq0T[:, j % 4, :], ps[:, :], ACT.Copy).then_inc(rel["act"], 1)

            act.wait_ge(ld["vec"], 16)
            for b in range(B):
                ps = unit("yT0", b)[:, :].rearrange("p (k t) -> p k t", k=KC)
                for k in range(KC):
                    for dst in (yT_full[:, b, 256 * k:256 * k + 256], xT[0][:, k, SEQ * b:SEQ * b + SEQ]):
                        ins = nc.scalar.activation(dst, ps[:, k, :], ACT.Identity, bias=vecs[:, 1, k:k + 1],
                                                   scale=vecs[:, 0, k:k + 1])
                ins.then_inc(hi_done, 1)
                for k in range(KC):
                    ins = nc.scalar.activation(xrT[:, k, P * b:P * b + P], ps[:, k, P:2 * P], ACT.Identity,
                                               scale=vecs[:, 2, k:k + 1])
                ins.then_inc(rel["act"], 1)
            ps = unit("ffn0T")
            nc.scalar.activation(ffn0T[:, :, :], ps[:, :].rearrange("p (k n) -> p k n", k=KC),
                                 ACT.Copy).then_inc(rel["act"], 1)
            act.wait_ge(e_in, 1)
            nc.scalar.activation(small[:, 1, :], small[:, 0, :], ACT.Exp).then_inc(e_out, 1)

            def qkv_hi(j):
                ps = unit("qkvT", j)
                nc.scalar.activation(qkvT[0][:, :, 256 * j:256 * j + 256], ps[:, :].rearrange("p (k n) -> p k n", k=KC),
                                     ACT.Copy).then_inc(hi_done, 1)

            for j in range(5):
                qkv_hi(j)
            ps = unit("probT0")
            nc.scalar.activation(probT0[0:2 * H, :], ps[0:2 * H, :], ACT.Copy).then_inc(rel["act"], 1)
            for j in range(5, QKV1 // 256):
                qkv_hi(j)
            for j in range(FF // 256):
                ps = unit("fcT", j)
                nc.scalar.activation(fcT[:, :, 256 * j:256 * j + 256], ps[:, :].rearrange("p (k n) -> p k n", k=KC),
                                     ACT.Copy).then_inc(rel["act"], 1)
            for j in range(FF // 256):
                ps = unit("projT", j)
                nc.scalar.activation(projT[:, 2 * j:2 * j + 2, :], ps[:, :].rearrange("p (k n) -> p k n", k=2),
                                     ACT.Copy).then_inc(rel["act"], 1)
            for b in range(B):
                ps = unit("yT1", b)[:, :].rearrange("p (k e t) -> p k t e", k=KC, e=2)
                for k in range(KC):
                    ins = nc.scalar.activation(xT[0][:, k, SEQ * b:SEQ * b + SEQ].rearrange("p (t e) -> p t e", e=2),
                                               ps[:, k, :, :], ACT.Copy)
                ins.then_inc(hi_done, 1)

            def gelu(t):
                act.wait_ge(f_fc, t + 1)
                for half in range(2):
                    ins = nc.scalar.activation(ffn_h[:, t % 2, 512 * half:512 * half + 512],
                                               bank[2 * (t % 2) + half][:, :], ACT.Gelu, scale=ffac[:, t, 0:1])
                ins.then_inc(f_gelu, 1)

            act.wait_ge(f_fac, 1)
            gelu(0)
            gelu(1)
            for t in range(8):
                act.wait_ge(f_norm, t + 1)
                nc.scalar.activation(ffn_h[:, t % 2, :], ffn_h[:, t % 2, :], ACT.Identity, bias=ffac[:, t, 4:5],
                                     scale=ffac[:, t, 3:4]).then_inc(f_y, 1)
                if t + 2 < 8:
                    gelu(t + 2)
                for half in range(2):
                    act.wait_ge(f_T, 2 * t + half + 1)
                    nc.scalar.activation(hT[t % 2][0][:, 4 * half:4 * half + 4, :],
                                         bank[4 + half][:, :].rearrange("p (k n) -> p k n", k=4),
                                         ACT.Copy).then_inc(f_hi, 1)
                if t < 4:
                    for j in (2 * t, 2 * t + 1):
                        act.wait_ge(wo_full, j + 1)
                        nc.scalar.activation(woT[0][:, 2 * j:2 * j + 2, :], bank[7][:, :].rearrange("p (k n) -> p k n", k=2),
                                             ACT.Copy).then_inc(wo_hi, 1)

            def hi_lo_T(what, it, kind, par):
                b, n = place(what, it, kind)
                act.wait_ge(full[b], n + 1)
                if what == "kT":
                    dst = kT[par][:, :, :]
                    src = bank[b][:, :].rearrange("p (s t) -> p s t", s=2)
                else:
                    j = int(what[2])
                    c, h = j // 2, 4 * (j % 2)
                    dst = qT[par][:, h:h + 4, P * c:P * c + P]
                    src = bank[b][:, :].rearrange("p (h t) -> p h t", h=4)
                nc.scalar.activation(dst, src, ACT.Copy).then_inc(free[b], 1)

            def probs(it, u, par, kind):
                n = it * UNITS + u
                if u >= 3 or kind != FIRST:
                    act.wait_ge(t_full, n - 2)
                act.wait_ge(s_max, n + 1)
                heads, h, wide = unit_heads(u)
                h += 8 * (u >= 2)
                for j in range(heads):
                    ins = nc.scalar.activation(prob[u % 3][:, wide * j:wide * j + wide], bank[u % 2][:, wide * j:wide * j + wide],
                                               ACT.Exp, bias=neg_max[par][:, h + j:h + j + 1],
                                               accum_out=sums[par][:, h + j:h + j + 1])
                ins.then_inc(s_exp, 1)

            def probs_T(it, u, early=False):
                n = it * UNITS + u
                act.wait_ge(t_full, n + 1)
                if not early:
                    act.wait_ge(pv_done, n - 2)
                nc.scalar.activation(probT[u % 3][:, :], bank[2 + u % 2][:, :], ACT.Copy).then_inc(t_done, 1)

            def heads_T(c, it, kind):
                b, n = place(f"oT{c}", it, kind)
                act.wait_ge(full[b], n + 1)
                nc.scalar.activation(oT[0][:, :, P * c:P * c + P], bank[b][:, :].rearrange("p (c t) -> p c t", c=4),
                                     ACT.Copy).then_inc(oT_hi, 1)

            def iteration(it, par, kind):
                for u in range(UNITS):
                    if u >= 2:
                        probs_T(it, u - 2, early=kind == FIRST and u < 5)
                    elif kind != FIRST:
                        probs_T(it - 1, u + 4)
                    probs(it, u, par, kind)
                    if u == 1 and kind != FIRST:
                        heads_T(0, it, kind)
                    if kind != LAST and u == 3:
                        hi_lo_T("qT0", it, kind, 1 - par)
                        hi_lo_T("qT1", it, kind, 1 - par)
                    if kind != LAST and u == 4:
                        hi_lo_T("qT2", it, kind, 1 - par)
                    if u == 4 and kind != FIRST:
                        heads_T(1, it, kind)
                    if kind != LAST and u == 4:
                        hi_lo_T("qT3", it, kind, 1 - par)
                    if kind != LAST and u == 5:
                        hi_lo_T("kT", it, kind, 1 - par)

            for what in ("qT0", "qT1", "qT2", "qT3", "kT"):
                hi_lo_T(what, -1, BEFORE, 0)
            iterations(act, iteration)
            for u in (4, 5):
                probs_T(ITS - 1, u)
            for c in range(2):
                heads_T(c, ITS, AFTER)

        @block.gpsimd
        def _(pool):
            pool.memset(blk_k[:, :, :, :], 0.0).then_inc(zeroed, 1)
            pool.memset(blk_v[:, :], 0.0).then_inc(zeroed, 1)
            pool.wait_ge(zeroed, 2)
            pool.memset(probT0[2 * H:2 * H + 1, :], 1.0).then_inc(zeroed, 1)
            pool.wait_ge(zeroed, 3)
            pool.memset(neg_half[:, :], -0.5).then_inc(zeroed, 1)
            pool.wait_ge(zeroed, 4)
            r, ms, c1, c2, rc, f1 = (tok[:, i, :] for i in range(6))

            def root(a, n):
                pool.wait_ge(root_in, n)
                pool.tensor_tensor(a, a, neg_half[:, 0:a.shape[1]], ALU.pow).then_inc(root_out, 1)

            def own(ins, n):
                ins.then_inc(s_pool, 1)
                pool.wait_ge(s_pool, n)

            for n, a in enumerate([r, c1, c2]):
                root(a, n + 1)
            pool.wait_ge(inv1, 1)
            w = nat_proj[:, :, :]
            own(pool.tensor_scalar(w, w, winv[:, 2:3], MAGIC, ALU.mult, ALU.add), 1)
            own(pool.tensor_scalar(w, w, -MAGIC, 1.0, ALU.add, ALU.mult), 2)
            pool.tensor_scalar(w, w, 1.0, -1.0, ALU.min, ALU.max).then_inc(tern_proj, 1)
            OWN0, OWN = 2, 3
            for n, a in enumerate([r, c2]):
                root(a, n + 4)

            def sequence(it):
                for s in range(2):
                    ins = pool.tensor_copy(xb[s][:, :, :].rearrange("p (k c) t -> p k (c t)", k=KC),
                                           xT[s][:, :, bass.ds((it // HKV) * SEQ, SEQ)])
                ins.then_inc(xb_done, 1)

            def queries(it, kind, n):
                for c in range(2):
                    b, m = place(f"q{c}", it, kind)
                    pool.wait_ge(free[b], m + 1)
                    if c == 0 and kind != BEFORE:
                        if kind == FIRST:
                            pool.wait_ge(full[6], place("kT", -1, BEFORE)[1] + 1)
                            pool.wait_ge(full[7], place("qT3", -1, BEFORE)[1] + 1)
                        else:
                            pool.wait_ge(full[6], it * 6 + 2)
                            pool.wait_ge(full[7], it * 6 + 2)
                    hi, lo = (q_nat[:, c, :, s, :] for s in range(2))
                    terms = [a.rearrange("p (h d) -> p h d", h=HG) for a in (rope_a[:, c, :], rope_b[:, c, :])]
                    pool.tensor_tensor(hi.bitcast(F32R), *terms, ALU.add)
                    own(pool.tensor_tensor(terms[0], *terms, ALU.add), n + c + 1)
                    pool.tensor_tensor(lo, terms[0], hi, ALU.subtract).then_inc(qn_done, 1)

            def keys(it, kind, n):
                b, m = place("kv", it, kind)
                pool.wait_ge(free[b], m + 1)
                k1, k2 = rope_k[:, 0, :, :], rope_k[:, 1, :, :]
                for w in range(2):
                    pool.tensor_tensor(k_nat[:, 0, :, w, :].bitcast(F32R), k1, k2, ALU.add)
                own(pool.tensor_tensor(k1, k1, k2, ALU.add), n + 3)
                for w in range(2):
                    ins = pool.tensor_tensor(k_nat[:, 1, :, w, :], k1, k_nat[:, 0, :, w, :], ALU.subtract)
                ins.then_inc(kn_done, 1)

            pool.wait_ge(rel["dve"], released("dve", len(ORDER) - 1))
            sequence(0)
            for t in range(8):
                root(ffac[:, t, 1:2], t + 6)

            def prepare(it, kind, n, more):
                queries(it, kind, n)
                keys(it, kind, n)
                if more:
                    sequence(it + 2)

            prepare(-1, BEFORE, OWN0, True)
            prepare(0, FIRST, OWN0 + OWN, True)
            with pool.Fori(1, ITS - 2) as it:
                prepare(it, INNER, OWN0 + OWN * (it + 1), True)
            prepare(ITS - 2, INNER, OWN0 + OWN * (ITS - 1), False)

        @block.vector
        def _(dve):
            count = [0]

            def link(ins):
                count[0] += 1
                ins.then_inc(s_dve, 1)
                dve.wait_ge(s_dve, count[0])

            roots = [0]

            def ask(dst, src, eps):
                roots[0] += 1
                dve.tensor_scalar(dst, src, eps, None, ALU.add).then_inc(root_in, 1)

            def rooted():
                dve.wait_ge(root_out, roots[0])

            def unit(what, j=0):
                n = UNIT[(what, j)]
                dve.wait_ge(filled, n + 1)
                return bank[n % RING]

            def layer_stats():
                for t in range(8):
                    ins = dve.bn_stats(stats[:, t, :], x[:, t // 2, t % 2, :])
                link(ins)
                for t in range(8):
                    ins = dve.bn_aggr(mv[:, t, :], stats[:, t, :])
                link(ins)

            r, ms, c1, c2, rc, f1 = (tok[:, i, :] for i in range(6))
            mean, var = mv[:, :, 0], mv[:, :, 1]

            dve.wait_ge(ld["x"], 16)
            layer_stats()
            ask(r, var, EPS_LN)
            dve.wait_ge(ld["cst"], 16)
            dve.tensor_copy(ident_b[:, :], ident)
            for j in range(4):
                ins = dve.tensor_copy(mask_b[:, j, :], cst[:, C_MASK:C_MASK + P])
            ins.then_inc(const_done, 1)
            rooted()
            link(dve.tensor_tensor(ms, r, r, ALU.mult))
            link(dve.tensor_tensor(ms, ms, var, ALU.mult))
            ask(c1, ms, EPS_RMS)
            ask(c2, ms, EPS_LN)
            dve.wait_ge(ld["ffn0"], 16)
            dve.tensor_reduce(wsum[:, 0:1], nat_ffn0[:, :, :], AX.XY, ALU.add, apply_absolute_value=True).then_inc(sum0_in, 1)
            rooted()
            link(dve.tensor_tensor(rc, r, c2, ALU.mult))
            for t in range(8):
                ins = dve.tensor_scalar(y0[:, t // 2, t % 2, :], x[:, t // 2, t % 2, :], mean[:, t:t + 1], rc[:, t:t + 1],
                                        ALU.subtract, ALU.mult)
                if t % 2:
                    ins.then_inc(y0_done, 1)

            def ternary(w, inverse):
                link(dve.tensor_scalar(w, w, inverse, MAGIC, ALU.mult, ALU.add))
                link(dve.tensor_scalar(w, w, MAGIC, 1.0, ALU.subtract, ALU.min))
                return dve.tensor_scalar(w, w, -1.0, None, ALU.max)

            dve.wait_ge(sum0_out, 1)
            link(dve.tensor_scalar(winv[:, 0:1], bank[7][:, 0:1], 1.0 / (DIM * DIM), 1e-5, ALU.mult, ALU.add))
            link(dve.reciprocal(winv[:, 0:1], winv[:, 0:1]))
            ternary(nat_ffn0[:, :, :], winv[:, 0:1]).then_inc(tern0, 1)
            link(dve.reciprocal(f1, c2))
            link(dve.tensor_tensor(f1, f1, c1, ALU.mult))
            link(dve.tensor_scalar(f1, f1, DH ** -0.5, None, ALU.mult))
            dve.wait_ge(g_mm, HC // 2)
            dve.tensor_copy(g0[:, :, :], bank[6][:, 0:2 * P].rearrange("p (k n) -> p k n", k=KC)[:, :, 0:2 * H]).then_inc(g_done, 1)

            for b in range(B):
                dve.wait_ge(hi_done, b + 1)
                at = slice(SEQ * b, SEQ * b + SEQ)
                dve.tensor_tensor(xT[1][:, :, at], yT_full[:, b, :].rearrange("p (k t) -> p k t", k=KC),
                                  xT[0][:, :, at].bitcast(F32), ALU.subtract).then_inc(lo0_done, 1)
            dve.wait_ge(m_full, 1)
            dve.tensor_copy(m0[0:2 * H, :], bank[6][0:2 * H, 0:DIM]).then_inc(m_done, 1)

            ps = unit("score0")
            for b in range(B):
                at = slice(2 * H * b, 2 * H * b + 2 * H)
                ins = dve.tensor_scalar(small[:, 3, at], ps[:, at], f1[:, 2 * b + 1:2 * b + 2], None, ALU.mult)
            ins.then_inc(rel["dve"], 1)
            dve.wait_ge(rel["dve"], released("dve", UNIT[("score0", 0)]))
            pair = small[:, :, :].rearrange("p w (n j) -> p w n j", j=2)
            top = small[:, 2, 0:H * B]
            link(dve.tensor_tensor(top, pair[:, 3, :, 0], pair[:, 3, :, 1], ALU.max))
            for j in range(2):
                ins = dve.tensor_tensor(pair[:, 0, :, j], pair[:, 3, :, j], top, ALU.subtract)
            ins.then_inc(e_in, 1)
            dve.wait_ge(e_out, 1)
            link(dve.tensor_tensor(top, pair[:, 1, :, 0], pair[:, 1, :, 1], ALU.add))
            link(dve.reciprocal(top, top))
            for j in range(2):
                ins = dve.tensor_tensor(pair[:, 3, :, j], pair[:, 1, :, j], top, ALU.mult)
            ins.then_inc(prob0, 1)

            def qkv_lo(j):
                ps = unit("qkvT", j)
                at = slice(256 * j, 256 * j + 256)
                dve.wait_ge(hi_done, B + j + 1)
                dve.tensor_tensor(qkvT[1][:, :, at], ps[:, :].rearrange("p (k n) -> p k n", k=KC),
                                  qkvT[0][:, :, at].bitcast(F32), ALU.subtract).then_inc(rel["dve"], 1)

            for j in range(5):
                qkv_lo(j)
            dve.wait_ge(ld["fc"], 16)
            dve.wait_ge(ld["proj"], 16)
            dve.tensor_reduce(wsum[:, 1:2], nat_fc[:, :, :], AX.XY, ALU.add, apply_absolute_value=True)
            dve.tensor_reduce(wsum[:, 2:3], nat_proj[:, :, :], AX.XY, ALU.add, apply_absolute_value=True).then_inc(sum1_in, 1)

            for b in range(B):
                ps = unit("out0", b)
                dve.tensor_tensor(x[:, b, :, :], x[:, b, :, :], ps[:, :].rearrange("p (e n) -> p e n", e=2),
                                  ALU.add).then_inc(rel["dve"], 1)
            dve.wait_ge(rel["dve"], released("dve", UNIT[("out0", B - 1)]))
            layer_stats()
            ask(r, var, EPS_LN)
            dve.wait_ge(sum1_out, 1)
            link(dve.tensor_scalar(wscale[:, 1:3], bank[7][:, 0:2], 1.0 / (DIM * FF), None, ALU.mult))
            link(dve.tensor_scalar(winv[:, 1:3], wscale[:, 1:3], EPS_BIT, None, ALU.add))
            dve.reciprocal(winv[:, 1:3], winv[:, 1:3]).then_inc(inv1, 1)
            for j in range(5, QKV1 // 256):
                qkv_lo(j)
            dve.wait_ge(inv1, 1)
            ternary(nat_fc[:, :, :], winv[:, 1:2]).then_inc(tern_fc, 1)
            rooted()
            for t in range(8):
                ins = dve.tensor_scalar(y1[:, t // 2, t % 2, :], x[:, t // 2, t % 2, :], mean[:, t:t + 1], r[:, t:t + 1],
                                        ALU.subtract, ALU.mult)
                if t % 2:
                    ins.then_inc(y1_done, 1)
            link(dve.tensor_tensor(ms, r, r, ALU.mult))
            link(dve.tensor_tensor(ms, ms, var, ALU.mult))
            ask(c2, ms, EPS_BIT)
            link(dve.reciprocal(f1, ms))
            link(dve.tensor_tensor(f1, f1, ms, ALU.mult))
            rooted()
            link(dve.tensor_tensor(c2, c2, f1, ALU.mult))
            dve.tensor_scalar(ffac[:, :, 0], c2, wscale[:, 1:2], None, ALU.mult).then_inc(f_fac, 1)
            for b in range(B):
                ps = unit("yT1", b)[:, :].rearrange("p (k e t) -> p k t e", k=KC, e=2)
                dve.wait_ge(hi_done, B + QKV1 // 256 + b + 1)
                for k in range(KC):
                    at = slice(SEQ * b, SEQ * b + SEQ)
                    ins = dve.tensor_tensor(xT[1][:, k, at].rearrange("p (t e) -> p t e", e=2), ps[:, k, :, :],
                                            xT[0][:, k, at].bitcast(F32).rearrange("p (t e) -> p t e", e=2), ALU.subtract)
                ins.then_inc(rel["dve"], 1)

            def hidden_stats(t):
                dve.wait_ge(f_gelu, t + 1)
                dve.bn_stats(fstat[:, t, 0:6], ffn_h[:, t % 2, 0:512])
                link(dve.bn_stats(fstat[:, t, 6:12], ffn_h[:, t % 2, 512:1024]))
                link(dve.bn_aggr(fmv[:, t, :], fstat[:, t, :]))
                fm, fv = fmv[:, t, 0:1], fmv[:, t, 1:2]
                ask(ffac[:, t, 1:2], fv, EPS_BIT)
                link(dve.reciprocal(ffac[:, t, 2:3], fv))
                link(dve.tensor_tensor(ffac[:, t, 2:3], ffac[:, t, 2:3], fv, ALU.mult))

            def hidden_factors(t):
                rooted()
                link(dve.tensor_scalar(ffac[:, t, 3:4], ffac[:, t, 1:2], ffac[:, t, 2:3], wscale[:, 2:3], ALU.mult, ALU.mult))
                dve.tensor_scalar(ffac[:, t, 4:5], ffac[:, t, 3:4], fmv[:, t, 0:1], -1.0, ALU.mult, ALU.mult).then_inc(f_norm, 1)

            def hidden_lo(t):
                for half in range(2):
                    dve.wait_ge(f_hi, 2 * t + half + 1)
                    dve.tensor_tensor(hT[t % 2][1][:, 4 * half:4 * half + 4, :], bank[4 + half][:, :].rearrange("p (k n) -> p k n", k=4),
                                      hT[t % 2][0][:, 4 * half:4 * half + 4, :].bitcast(F32), ALU.subtract).then_inc(f_lo, 1)

            def ffn_add(t):
                dve.wait_ge(f_out, t + 1)
                dve.tensor_tensor(x[:, t // 2, t % 2, :], x[:, t // 2, t % 2, :], bank[PROJ_BANK[t]][:, 0:DIM],
                                  ALU.add).then_inc(f_add, 1)

            hidden_stats(0)
            hidden_factors(0)
            for t in range(7):
                hidden_stats(t + 1)
                hidden_lo(t)
                hidden_factors(t + 1)
                if t < 4:
                    for j in (2 * t, 2 * t + 1):
                        dve.wait_ge(wo_hi, j + 1)
                        dve.tensor_tensor(woT[1][:, 2 * j:2 * j + 2, :], bank[7][:, :].rearrange("p (k n) -> p k n", k=2),
                                          woT[0][:, 2 * j:2 * j + 2, :].bitcast(F32), ALU.subtract).then_inc(wo_lo, 1)
                if t >= 1:
                    ffn_add(t - 1)

            def rope_q(c, it, kind):
                b, n = place(f"q{c}", it, kind)
                dve.wait_ge(full[b], n + 1)
                if kind != BEFORE:
                    dve.wait_ge(qn_done, it * 2 + c + 1)
                q = bank[b][:, :].rearrange("p (h s d) -> p h s d", h=HG, s=2)
                cos = cst[:, C_QC + DH * c:C_QC + DH * c + DH].rearrange("p (a n) -> p a n", a=1).to_broadcast([P, HG, DH])
                sin = cst[:, C_QS + DH * c:C_QS + DH * c + DH].rearrange("p (a s d) -> p a s d", a=1, s=2)
                dve.tensor_tensor(rope_a[:, c, :].rearrange("p (h d) -> p h d", h=HG),
                                  bank[b][:, :].rearrange("p (h d) -> p h d", h=HG), cos, ALU.mult)
                b4 = rope_b[:, c, :].rearrange("p (h s d) -> p h s d", h=HG, s=2)
                for s in range(2):
                    ins = dve.tensor_tensor(b4[:, :, s, :], q[:, :, 1 - s, :],
                                            sin[:, :, s, :].to_broadcast([P, HG, DH // 2]), ALU.mult)
                ins.then_inc(free[b], 1)

            def rope_kv(it, kind, par):
                b, n = place("kv", it, kind)
                dve.wait_ge(full[b], n + 1)
                if kind != BEFORE:
                    dve.wait_ge(kn_done, it + 1)
                kv = bank[b][:, 0:2 * P].rearrange("p (c w d) -> p c w d", c=2, w=2)
                cos = cst[:, C_KC:C_KC + P].rearrange("p (c d) -> p c d", c=2)
                sin = cst[:, C_KS:C_KS + P].rearrange("p (c s d) -> p c s d", c=2, s=2)
                dve.tensor_tensor(rope_k[:, 0, :, :], kv[:, :, 0, :], cos, ALU.mult)
                for s in range(2):
                    d = DH // 2
                    dve.tensor_tensor(rope_k[:, 1, :, d * s:d * s + d], kv[:, :, 0, d * (1 - s):d * (1 - s) + d],
                                      sin[:, :, s, :], ALU.mult)
                dve.tensor_copy(v[par][:, :, :], kv[:, :, 1, :]).then_inc(free[b], 1)

            rope_q(0, -1, BEFORE)
            rope_q(1, -1, BEFORE)
            hidden_lo(7)
            ffn_add(6)
            rope_kv(-1, BEFORE, 0)
            ffn_add(7)

            def maxima(it, u, par):
                dve.wait_ge(s_full, it * UNITS + u + 1)
                heads, h, _ = unit_heads(u)
                h += 8 * (u >= 2)
                dve.tensor_reduce(neg_max[par][:, h:h + heads], bank[u % 2][:, :].rearrange("p (h k) -> p h k", h=heads),
                                  AX.X, ALU.max, negate=True).then_inc(s_max, 1)

            def normalise(it, c, par):
                dve.wait_ge(pv_done, it * UNITS + (2 if c == 0 else 6))
                dve.reciprocal(rsum[par][:, 8 * c:8 * c + 8], sums[par][:, 8 * c:8 * c + 8]).then_inc(rs_done, 1)
                dve.wait_ge(rs_done, it * 2 + c + 1)
                dve.tensor_tensor(o_n[:, c, :].rearrange("p (h d) -> p h d", h=HG),
                                  bank[4 + c][:, :].rearrange("p (h d) -> p h d", h=HG),
                                  rsum[par][:, 8 * c:8 * c + 8].rearrange("p (h a) -> p h a", a=1).to_broadcast([P, HG, DH]),
                                  ALU.mult).then_inc(normed, 1)

            def heads_lo(c, it, kind):
                b, n = place(f"oT{c}", it, kind)
                dve.wait_ge(oT_hi, it * 2 - 1 + c)
                dst = slice(P * c, P * c + P)
                dve.tensor_tensor(oT[1][:, :, dst], bank[b][:, :].rearrange("p (c t) -> p c t", c=4),
                                  oT[0][:, :, dst].bitcast(F32), ALU.subtract).then_inc(free[b], 1)

            def add_out(e, it, kind):
                b, n = place(f"wo{e}", it, kind)
                dve.wait_ge(full[b], n + 1)
                dst = x[:, bass.ds((it - 1) // HKV, 1), e, :]
                dve.tensor_tensor(dst, dst, bank[b][:, 0:DIM].rearrange("p (a n) -> p a n", a=1), ALU.add).then_inc(free[b], 1)

            def iteration(it, par, kind):
                maxima(it, 0, par)
                if kind != LAST:
                    rope_q(0, it, kind)
                maxima(it, 1, par)
                if kind != FIRST:
                    heads_lo(0, it, kind)
                if kind != LAST:
                    rope_q(1, it, kind)
                maxima(it, 2, par)
                if kind != FIRST:
                    normalise(it - 1, 1, 1 - par)
                if kind != LAST:
                    rope_kv(it, kind, 1 - par)
                maxima(it, 3, par)
                maxima(it, 4, par)
                normalise(it, 0, par)
                if kind != FIRST:
                    heads_lo(1, it, kind)
                maxima(it, 5, par)
                if kind != FIRST:
                    add_out(0, it, kind)
                    add_out(1, it, kind)

            iterations(dve, iteration)
            normalise(ITS - 1, 1, 1)
            heads_lo(0, ITS, AFTER)
            heads_lo(1, ITS, AFTER)
            for e in range(2):
                add_out(e, ITS, AFTER)

        @block.tensor
        def _(pe):
            def ring(what, j=0):
                n = UNIT[(what, j)]
                if n >= RING:
                    engine = RELEASES[ORDER[n - RING][0]]
                    pe.wait_ge(rel[engine], released(engine, n - RING))
                return bank[n % RING]

            def transposes(ps, blocks):
                for j, a in enumerate(blocks):
                    ins = pe.transpose(ps[:, P * j:P * j + P], a, ident)
                return ins

            pe.wait_ge(ld["cst"], 16)
            ones = cst[:, C_ONE:C_ONE + P]
            pe.wait_ge(ld["pm"], 64)
            for w in range(2):
                for j in range(2):
                    col = (2 * w + j) * H
                    ins = pe.transpose(bank[6][:, col:col + H], pmn[:, w, j, :, :].rearrange("p a d -> p (a d)"), cst[0:H, C_ID:C_ID + H])
            ins.then_inc(pm_full, 1)

            def g_products(j):
                pe.wait_ge(rel["act"], released("act", UNIT[("wq0T", j)]))
                for i in range(2):
                    c = 2 * j + i
                    for k in range(KC):
                        col = P * k + 4 * c
                        ins = pe.matmul(bank[6][:, col:col + 4], wq0T[:, j % 4, 256 * i + P * k:256 * i + P * k + P],
                                        blk_k[:, c, :, :].rearrange("p s j -> p (s j)"), start=True, stop=True)
                ins.then_inc(g_mm, 1)

            pe.wait_ge(ld["wq0"], 16)
            for j in range(HC // 2):
                ps = ring("wq0T", j)
                transposes(ps, [wq0[:, k, P * c:P * c + P] for c in (2 * j, 2 * j + 1) for k in range(KC)]).then_inc(filled, 1)
                if j == 1:
                    pe.wait_ge(blk_done, 1)
                if j >= 1:
                    g_products(j - 1)
            pe.wait_ge(sum0_in, 1)
            pe.matmul(bank[7][:, 0:1], ones, wsum[:, 0:1], start=True, stop=True).then_inc(sum0_out, 1)
            g_products(HC // 2 - 1)

            for b in range(B):
                ps = ring("yT0", b)
                pe.wait_ge(y0_done, b + 1)
                transposes(ps, [y0[:, b, e, P * k:P * k + P] for k in range(KC) for e in range(2)]).then_inc(filled, 1)
            ps = ring("ffn0T")
            pe.wait_ge(tern0, 1)
            transposes(ps, [nat_ffn0[:, o, P * k:P * k + P] for k in range(KC) for o in range(2)]).then_inc(filled, 1)
            pe.wait_ge(ld["wout"], 16)
            pe.wait_ge(g_done, 1)
            for c in range(HC):
                ins = pe.matmul(bank[6][0:2 * H, 0:DIM], blk_v[:, 64 * c:64 * c + 64], wout0[:, c, :],
                                start=c == 0, stop=c == HC - 1)
            ins.then_inc(m_full, 1)
            ps = ring("score0")
            pe.wait_ge(rel["act"], released("act", UNIT[("yT0", B - 1)]))
            for b in range(B):
                for k in range(KC):
                    ins = pe.matmul(ps[:, 2 * H * b:2 * H * b + 2 * H], xrT[:, k, P * b:P * b + P], g0[:, k, :],
                                    start=k == 0, stop=k == KC - 1)
            ins.then_inc(filled, 1)

            def qkv_T(j):
                ps = ring("qkvT", j)
                transposes(ps, [nat_qkv[:, c, P * k:P * k + P] for k in range(KC) for c in (2 * j, 2 * j + 1)]).then_inc(filled, 1)

            pe.wait_ge(ld["qkv"], 16)
            for j in range(5):
                qkv_T(j)
            ps = ring("probT0")
            pe.wait_ge(prob0, 1)
            for b in range(B):
                ins = pe.transpose(ps[0:2 * H, P * b:P * b + P], small[:, 3, 2 * H * b:2 * H * b + 2 * H], ident)
            ins.then_inc(filled, 1)

            pe.wait_ge(m_done, 1)
            pe.wait_ge(lo0_done, B)
            pe.wait_ge(ld["bias"], 16)
            for b in range(B):
                ps = ring("out0", b)
                if b == 0:
                    pe.wait_ge(rel["act"], released("act", UNIT[("probT0", 0)]))
                for e in range(2):
                    o = ps[:, DIM * e:DIM * e + DIM]
                    p = probT0[:, P * b:P * b + P] if e else cst[0:2 * H + 1, C_EVEN:C_EVEN + P]
                    pe.matmul(o, p, m0[:, :], start=True, stop=False)
                    for k in range(KC):
                        for s in range(2):
                            col = SEQ * b + P * e
                            ins = pe.matmul(o, xT[s][:, k, col:col + P], ffn0T[:, k, :], start=False,
                                            stop=k == KC - 1 and s == 1)
                ins.then_inc(filled, 1)
            pe.wait_ge(sum1_in, 1)
            pe.matmul(bank[7][:, 0:2], ones, wsum[:, 1:3], start=True, stop=True).then_inc(sum1_out, 1)
            for j in range(5, QKV1 // 256):
                qkv_T(j)
            pe.wait_ge(tern_fc, 1)
            for j in range(FF // 256):
                ps = ring("fcT", j)
                transposes(ps, [nat_fc[:, c, P * k:P * k + P] for k in range(KC) for c in (2 * j, 2 * j + 1)]).then_inc(filled, 1)
            pe.wait_ge(tern_proj, 1)
            for j in range(FF // 256):
                ps = ring("projT", j)
                transposes(ps, [nat_proj[:, k, P * c:P * c + P] for c in (2 * j, 2 * j + 1) for k in range(2)]).then_inc(filled, 1)
            for b in range(B):
                ps = ring("yT1", b)
                pe.wait_ge(y1_done, b + 1)
                transposes(ps, [y1[:, b, e, P * k:P * k + P] for k in range(KC) for e in range(2)]).then_inc(filled, 1)

            def fc(t):
                if t >= 2:
                    pe.wait_ge(f_gelu, t - 1)
                col = SEQ * (t // 2) + t % 2
                for half in range(2):
                    n = 0
                    for k in range(KC):
                        for s in range(2):
                            ins = pe.matmul(bank[2 * (t % 2) + half][:, :], xT[s][:, k, col:col + 2 * P - 1:2],
                                            fcT[:, k, 512 * half:512 * half + 512], start=n == 0, stop=n == 3)
                            n += 1
                ins.then_inc(f_fc, 1)

            def hidden_T(t):
                pe.wait_ge(f_y, t + 1)
                for half in range(2):
                    if t >= 1:
                        pe.wait_ge(f_lo, 2 * (t - 1) + half + 1)
                    transposes(bank[4 + half], [ffn_h[:, t % 2, P * k:P * k + P] for k in range(4 * half, 4 * half + 4)]
                               ).then_inc(f_T, 1)

            def proj(t):
                pe.wait_ge(f_lo, 2 * t + 2)
                if PROJ_BANK[t] == 6 and t >= 1:
                    pe.wait_ge(f_add, t)
                if t == 7:
                    pe.wait_ge(f_add, 6)
                n = 0
                for k in range(FF // P):
                    for s in range(2):
                        ins = pe.matmul(bank[PROJ_BANK[t]][:, 0:DIM], hT[t % 2][s][:, k, :], projT[:, k, :],
                                        start=n == 0, stop=n == 2 * FF // P - 1)
                        n += 1
                ins.then_inc(f_out, 1)

            def w_o_T(j):
                if j >= 1:
                    pe.wait_ge(wo_lo, j)
                transposes(bank[7], [nat_o[:, k, P * c:P * c + P] for c in (2 * j, 2 * j + 1) for k in range(2)]).then_inc(wo_full, 1)

            W = [(0, 0), (1, 0), (0, 1)]

            def group_cols(w, k, it, what):
                g = (it + 1) % HKV
                if what == "q":
                    return w[:, k, bass.ds(g * (HG * DH), HG * DH)]
                kv = w[:, k, H * DH:QKV1].rearrange("p (w n) -> p w n", w=2)
                return kv[:, :, bass.ds(g * DH, DH)]

            def project_q(c, it, kind):
                b, n = place(f"q{c}", it, kind)
                if n > 0 or kind == INNER:
                    pe.wait_ge(free[b], n)
                if c == 0:
                    pe.wait_ge(xb_done, it + 2)
                i = 0
                for s, w in W:
                    for k in range(KC):
                        ins = pe.matmul(bank[b][:, :], xb[s][:, 2 * k + c, :], group_cols(qkvT[w], k, it, "q"), start=i == 0, stop=i == 5)
                        i += 1
                ins.then_inc(full[b], 1)

            def project_kv(it, kind):
                b, n = place("kv", it, kind)
                pe.wait_ge(free[b], n)
                for c in range(2):
                    i = 0
                    for s, w in W:
                        for k in range(KC):
                            ins = pe.matmul(bank[b][:, P * c:P * c + P].rearrange("p (w d) -> p w d", w=2), xb[s][:, 2 * k + c, :],
                                            group_cols(qkvT[w], k, it, "kv"), start=i == 0, stop=i == 5)
                            i += 1
                ins.then_inc(full[b], 1)

            def turn(what, it, kind):
                b, n = place(what, it, kind)
                pe.wait_ge(free[b], n)
                if what == "kT":
                    pe.wait_ge(kn_done, it + 2)
                    blocks = [k_nat[:, s, c, :, :].rearrange("p w d -> p (w d)") for s in range(2) for c in range(2)]
                else:
                    j = int(what[2])
                    c, h = j // 2, 4 * (j % 2)
                    pe.wait_ge(qn_done, it * 2 + 2 + c + 1)
                    blocks = [q_nat[:, c, h + i, :, :].rearrange("p s d -> p (s d)") for i in range(4)]
                transposes(bank[b], blocks).then_inc(full[b], 1)

            pe.wait_ge(rel["act"], released("act", len(ORDER) - 1))
            pe.wait_ge(rel["dve"], released("dve", len(ORDER) - 1))
            fc(0)
            fc(1)
            pe.wait_ge(ld["o"], 16)
            for t in range(8):
                hidden_T(t)
                if t + 2 < 8:
                    fc(t + 2)
                if t < 4:
                    w_o_T(2 * t)
                if t >= 1:
                    proj(t - 1)
                if t < 4:
                    w_o_T(2 * t + 1)
                if t == 6:
                    pe.wait_ge(f_add, 5)
                    pe.wait_ge(wo_lo, 8)
                    project_q(0, -1, BEFORE)
                    project_q(1, -1, BEFORE)
            project_kv(-1, BEFORE)
            proj(7)
            for what in ("qT0", "qT1", "qT2", "qT3", "kT"):
                turn(what, -1, BEFORE)

            def scores(it, u, par, kind):
                if u == 0:
                    for b in (6, 7):
                        pe.wait_ge(free[b], 4 if kind == FIRST else it * 6 + 1)
                if u >= 2 or kind != FIRST:
                    pe.wait_ge(s_exp, it * UNITS + u - 1)
                elif u == 0:
                    pe.wait_ge(f_add, 8)
                ps = bank[u % 2]
                heads, h, keys = unit_heads(u)
                c = 1 if u >= 2 else 0
                for j in range(heads):
                    for s in range(2):
                        pe.matmul(ps[:, keys * j:keys * j + keys], qT[par][:, h + j, P * c:P * c + P], kT[par][:, s, 0:keys],
                                  start=j == 0 and s == 0, stop=False, skip_group_check=True)
                diag = ps[:, :].rearrange("p (h k) -> p h k", h=heads)[:, :, P * c:P * c + P]
                pe.matmul(diag, ident_b[:, :], mask_b[:, 0:heads, :], start=False, stop=True,
                          skip_group_check=True).then_inc(s_full, 1)

            def prob_T(it, u, early=False):
                n = it * UNITS + u
                pe.wait_ge(s_exp, n + 1)
                if not early:
                    pe.wait_ge(t_done, n - 1)
                transposes(bank[2 + u % 2], [prob[u % 3][:, P * j:P * j + P] for j in range(4)]).then_inc(t_full, 1)

            def heads_out(it, u, par, first=False):
                n = it * UNITS + u
                pe.wait_ge(t_done, n + 1)
                if u in (0, 2) and not first:
                    pe.wait_ge(normed, it * 2 - (1 if u == 0 else 0))
                heads, h, _ = unit_heads(u)
                for j in range(heads):
                    col = DH * (h + j)
                    if u < 2:
                        ins = pe.matmul(bank[4][:, col:col + DH], probT[u % 3][:, P * j:P * j + P], v[par][:, 0, :], start=True, stop=True)
                    else:
                        for k in range(2):
                            ins = pe.matmul(bank[5][:, col:col + DH], probT[u % 3][:, P * (2 * j + k):P * (2 * j + k) + P], v[par][:, k, :],
                                            start=k == 0, stop=k == 1)
                ins.then_inc(pv_done, 1)

            def turn_heads(c, it, kind):
                b, n = place(f"oT{c}", it, kind)
                pe.wait_ge(free[b], n)
                pe.wait_ge(normed, it * 2 - 1 + c)
                transposes(bank[b], [o_n[:, c, P * j:P * j + P] for j in range(4)]).then_inc(full[b], 1)

            def project_out(e, it, kind):
                b, n = place(f"wo{e}", it, kind)
                pe.wait_ge(free[b], n)
                for c in range(2):
                    ob, on = place(f"oT{c}", it, kind)
                    pe.wait_ge(free[ob], on + 1)
                g = (it - 1) % HKV
                i = 0
                for s, w in W:
                    for j in range(4):
                        rhs = woT[w][:, bass.ds(g * 4 + j, 1), :].rearrange("p a n -> p (a n)")
                        ins = pe.matmul(bank[b][:, 0:DIM], oT[s][:, j, e:e + 2 * P - 1:2], rhs, start=i == 0, stop=i == 11)
                        i += 1
                ins.then_inc(full[b], 1)

            def iteration(it, par, kind):
                for u in range(UNITS):
                    scores(it, u, par, kind)
                    if u == 0 and kind != LAST:
                        project_q(0, it, kind)
                    if u >= 2:
                        prob_T(it, u - 2, early=kind == FIRST and u < 4)
                    elif kind != FIRST:
                        prob_T(it - 1, u + 4)
                    if u >= 3:
                        heads_out(it, u - 3, par, first=kind == FIRST)
                    elif kind != FIRST:
                        heads_out(it - 1, u + 3, 1 - par)
                    if u == 1:
                        if kind != FIRST:
                            turn_heads(0, it, kind)
                        if kind != LAST:
                            project_q(1, it, kind)
                    if u == 2 and kind != LAST:
                        project_kv(it, kind)
                    if u == 3 and kind != LAST:
                        turn("qT0", it, kind)
                        turn("qT1", it, kind)
                    if u == 4:
                        if kind != LAST:
                            turn("qT2", it, kind)
                        if kind != FIRST:
                            turn_heads(1, it, kind)
                        if kind != LAST:
                            turn("qT3", it, kind)
                    if u == 5:
                        if kind != LAST:
                            turn("kT", it, kind)
                        if kind != FIRST:
                            project_out(0, it, kind)
                            project_out(1, it, kind)
                if kind == FIRST:
                    pe.wait_ge(free[6], place("kT", it, kind)[1] + 1)
                    pe.wait_ge(free[7], place("qT3", it, kind)[1] + 1)

            pe.wait_ge(const_done, 1)
            iterations(pe, iteration)
            prob_T(ITS - 1, 4)
            heads_out(ITS - 1, 3, 1)
            prob_T(ITS - 1, 5)
            heads_out(ITS - 1, 4, 1)
            heads_out(ITS - 1, 5, 1)
            for c in range(2):
                turn_heads(c, ITS, AFTER)
            for e in range(2):
                project_out(e, ITS, AFTER)


_INS = ["L0_attn_seq", "L0_attn_w_qkv", "L0_attn_w_out", "L0_attn_pm", "L0_ffn_weight", "L0_ffn_bias",
        "L1_attn_w_qkv", "L1_attn_w_o", "L1_ffn_w_fc", "L1_ffn_w_proj"]
_VECS = ["L0_ffn_ln_gamma", "L0_ffn_ln_beta", "L0_attn_w_norm"]


def kernel(**inputs):
    import concourse.bacc as bacc
    from concourse.bass_utils import run_bass_kernel_spmd

    nc = bacc.Bacc("TRN2", target_bir_lowering=False, num_devices=1)
    arrays, args = {}, []
    for name in _INS:
        a = np.ascontiguousarray(inputs[name])
        arrays[f"in_{name}_dram"] = a
        args.append(nc.dram_tensor(f"in_{name}_dram", a.shape, mybir.dt.from_np(a.dtype), kind="ExternalInput").ap())
    arrays["vec_dram"] = np.ascontiguousarray(np.stack([np.asarray(inputs[n]).reshape(KC, P) for n in _VECS]).transpose(2, 0, 1))
    args.append(nc.dram_tensor("vec_dram", (P, len(_VECS), KC), F32, kind="ExternalInput").ap())
    arrays["const_dram"] = constants()
    args.append(nc.dram_tensor("const_dram", (P, C_ALL), F32, kind="ExternalInput").ap())
    args.append(nc.dram_tensor("out_0_dram", (B, SEQ, DIM), F32, kind="ExternalOutput").ap())
    build(nc, *args)
    r = run_bass_kernel_spmd(nc, [arrays], core_ids=[0])
    return r.results[0]["out_0_dram"]
```

```python
from contextlib import ExitStack

import numpy as np

import concourse.bass as bass
from concourse import mybir

F32 = mybir.dt.float32
F32R = mybir.dt.float32r
BF16 = mybir.dt.bfloat16
ALU = mybir.AluOpType
ACT = mybir.ActivationFunctionType
AX = mybir.AxisListType

P = 128
B, SEQ, DIM = 4, 256, 256
KC = DIM // P
H, DH = 32, 64
HKV = 4
HG = H // HKV
HC = H * DH // P
QKV1 = (H + 2 * HKV) * DH
FF = 4 * DIM
THETA = 10000.0
EPS_LN, EPS_BIT = 1e-5, 1e-6
EPS_RMS = float(np.finfo(np.float32).eps)
MAGIC = 1.5 * 2.0 ** 23
MASKED = -1e30
WQ0_PIECES = 4
RING = 6
ITS = B * HKV
UNITS = 6

C_ID, C_MASK, C_EVEN, C_ONE, C_QC, C_QS, C_KC, C_KS = (P * i for i in range(8))
C_ALL = 8 * P


def constants():
    c = np.zeros((P, C_ALL), np.float32)
    c[:, C_ID:C_ID + P] = np.eye(P)
    c[:, C_MASK:C_MASK + P] = np.where(np.arange(P)[None] > np.arange(P)[:, None], MASKED, 0.0)
    c[0:2 * H:2, C_EVEN:C_EVEN + P] = 1.0
    c[2 * H, C_EVEN:C_EVEN + P] = 1.0
    c[:, C_ONE:C_ONE + P] = 1.0
    inv = (1.0 / np.float32(THETA) ** (np.arange(0, DH, 2, dtype=np.float32) / np.float32(DH))).astype(np.float32)
    for t in range(2):
        ang = (np.arange(P, dtype=np.float32) + np.float32(P * t))[:, None] * inv[None]
        cos = np.cos(ang).astype(np.float32)
        sin = np.sin(ang).astype(np.float32)
        cc, ss = np.concatenate([cos, cos], 1), np.concatenate([-sin, sin], 1)
        at = DH * t
        c[:, C_QC + at:C_QC + at + DH] = cc * np.float32(DH ** -0.5)
        c[:, C_QS + at:C_QS + at + DH] = ss * np.float32(DH ** -0.5)
        c[:, C_KC + at:C_KC + at + DH] = cc
        c[:, C_KS + at:C_KS + at + DH] = ss
    return c


ORDER = ([("wq0T", j) for j in range(HC // 2)] + [("yT0", b) for b in range(B)]
         + [("ffn0T", 0), ("score0", 0)] + [("fcT", j) for j in range(FF // 256)]
         + [("qkvT", 0), ("probT0", 0), ("qkvT", 1)]
         + [("out0", 0), ("out0", 1), ("qkvT", 2), ("out0", 2), ("yT1", 0), ("out0", 3), ("yT1", 1), ("yT1", 2), ("yT1", 3)])
RING_QKV = 3
assert len(ORDER) % RING == 0
UNIT = {key: n for n, key in enumerate(ORDER)}
RELEASES = {"yT0": "act", "ffn0T": "act", "wq0T": "act", "score0": "dve", "qkvT": "dve", "probT0": "act",
            "out0": "dve", "fcT": "act", "yT1": "dve"}


HI = {u: sum(w in ("qkvT", "yT1") for w, _ in ORDER[:n + 1]) for u, n in UNIT.items()}


def released(engine, n):
    return sum(RELEASES[what] == engine for what, _ in ORDER[:n + 1])


def build(nc, seq, w_qkv0, w_out0, pm, w_ffn0, bias0, w_qkv1, w_o1, w_fc, w_proj, vec, const, out):
    with ExitStack() as ctx:
        def sb(name, shape, dt=F32):
            return ctx.enter_context(nc.sbuf_tensor(name, shape, dt))

        def sem(name):
            return ctx.enter_context(nc.semaphore(name))

        bank = [ctx.enter_context(nc.psum_tensor(f"bank{i}", [P, 512], F32)) for i in range(8)]

        cst = sb("cst", [P, C_ALL])
        ident = cst[:, C_ID:C_ID + P]
        ident_b = sb("ident_b", [P, P], BF16)
        mask_b = sb("mask_b", [P, 4, P], BF16)
        x = sb("x", [P, B, 2, DIM])
        stats = sb("stats", [P, 8, 6])
        mv = sb("mv", [P, 8, 2])
        tok = sb("tok", [P, 5, 8])
        fstat = sb("fstat", [P, 8, 12])
        fmv = sb("fmv", [P, 8, 2])
        ffac = sb("ffac", [P, 8, 8])
        vecs = sb("vecs", [P, 3, KC])
        neg_half = sb("neg_half", [P, 2, 8])
        wsum = sb("wsum", [P, 4])
        wscale = sb("wscale", [P, 4])
        winv = sb("winv", [P, 4])
        neg_magic = sb("neg_magic", [P, 1])
        table_use = sb("table_use", [P, 2])
        sums = [sb(f"sums{i}", [P, 16]) for i in range(2)]
        rsum = [sb(f"rsum{i}", [P, 16]) for i in range(2)]
        neg_max = [sb(f"neg_max{i}", [P, 16]) for i in range(2)]

        base = (nc.sbuf_base + 63) // 64 * 64
        ends = [0]

        def at(name, offset, shape, dt=F32):
            ends[0] = max(ends[0], offset + 4 * int(np.prod(shape[1:])))
            return nc.alloc_sbuf_tensor_at(name, shape, dt, offset=base + offset)

        K = 1024
        y0 = at("y0", 0, [P, B, 2, DIM])
        qkvT = [at(f"qkvT_{w}", 20 * K * i, [P, KC, QKV1], F32R) for i, w in enumerate(("hi", "lo"))]
        xT = [at(f"xT_{w}", 40 * K + 8 * K * i, [P, KC, B * SEQ], F32R) for i, w in enumerate(("hi", "lo"))]
        fcT = at("fcT", 56 * K, [P, KC, FF], F32R)
        projT = at("projT", 64 * K, [P, FF // P, DIM], F32R)
        woT = [at(f"woT_{w}", 72 * K + 16 * K * i, [P, HC, DIM], F32R) for i, w in enumerate(("hi", "lo"))]
        blk_v = at("blk_v", 72 * K, [P, HC * 68])
        small = at("small", 77 * K, [P, 4, 2 * H * B])
        probT0 = at("probT0", 81 * K, [2 * H + 1, B * P])
        xrT = at("xrT", 83 * K, [P, KC, B * P])
        wout0 = at("wout0", 88 * K, [P, HC, DIM])
        wq0 = at("wq0", 104 * K, [P, KC, H * DH])
        y1 = at("y1", 104 * K, [P, B, 2, DIM])
        ffn_h = [at(f"ffn_h{t}", k * K, [P, FF]) for t, k in enumerate((104, 112, 108, 116, 128, 132, 112, 116))]
        kT = [at(f"kT{i}", 104 * K + 2 * K * i, [P, 2, SEQ], F32R) for i in range(2)]
        k_nat = at("k_nat", 108 * K, [P, 2, 2, 2, DH])
        rope_k = at("rope_k", 110 * K, [P, 2, 2, DH])
        k_sum = at("k_sum", 111 * K, [P, 2, DH])
        oT = [[at(f"oT{i}_{w}", k * K + 4 * K * j, [P, 4, SEQ], F32R) for j, w in enumerate(("hi", "lo"))]
              for i, k in enumerate((112, 172))]
        nat_qkv = at("nat_qkv", 120 * K, [P, QKV1 // P, DIM])
        qT = [at(f"qT{i}", 120 * K + 8 * K * i, [P, HG, SEQ], F32R) for i in range(2)]
        q_raw = at("q_raw", 136 * K, [P, 2, 512])
        hT = [[at(f"hT{i}_{w}", 140 * K + 8 * K * i + 4 * K * j, [P, FF // P, P], F32R) for j, w in enumerate(("hi", "lo"))]
              for i in range(2)]
        prob = [at(f"prob{i}", 140 * K + 2 * K * i, [P, 512]) for i in range(3)]
        probT = [[at(f"probT{i}_{w}", (146 + 2 * i + 4 * j) * K, [P, 512], F32R) for j, w in enumerate(("hi", "lo"))]
                 for i in range(2)]
        yT_full = at("yT_full", 156 * K, [P, B, 512])
        q_nat = at("q_nat", 156 * K, [P, 2, HG, 2, DH])
        nat_proj = at("nat_proj", 164 * K, [P, 2, FF])
        rope_a = at("rope_a", 164 * K, [P, 2, 512])
        rope_b = at("rope_b", 168 * K, [P, 2, 512])
        nat_fc = at("nat_fc", 180 * K, [P, FF // P, DIM])
        nat_o = at("nat_o", 172 * K, [P, 2, H * DH])
        v = [at(f"v{i}", (188 + 2 * i) * K, [P, 2, 2, P], F32R) for i in range(2)]
        nat_ffn0 = at("nat_ffn0", 172 * K, [P, 2, DIM])
        ffn0T = at("ffn0T", 174 * K, [P, KC, DIM], F32R)
        pmn = at("pmn", 176 * K, [H, 2, 2, 2, DH])
        wq0T = at("wq0T", 140 * K, [P, 4, 512])
        m0 = at("m0", 148 * K, [2 * H + 1, DIM])
        gT = at("gT", 149 * K, [2 * H, DIM])
        g0 = at("g0", 150 * K, [P, KC, 2 * H])
        blk_k = at("blk_k", 151 * K, [P, HC * 68])
        assert base + ends[0] <= nc.sbuf_usable_end, (base, ends[0], nc.sbuf_usable_end)

        ld = {n: sem("ld_" + n) for n in ("x", "cst", "vec", "bias", "pm", "ffn0", "wout", "qkv", "o", "fc", "proj", "rope")}
        ld_wq0 = [sem(f"ld_wq0_{i}") for i in range(WQ0_PIECES)]
        s_dve, s_pool = sem("s_dve"), sem("s_pool")
        filled = sem("filled")
        rel = {"act": sem("rel_act"), "dve": sem("rel_dve")}
        full_done, x_hi = sem("full_done"), sem("x_hi")
        hi_done = sem("hi_done")
        root_in, root_out = sem("root_in"), sem("root_out")
        const_done = sem("const_done")
        y0_done, y1_done = sem("y0_done"), sem("y1_done")
        sum_in, sum_out = sem("sum_in"), sem("sum_out")
        tern0, tern_fc, tern_proj = sem("tern0"), sem("tern_fc"), sem("tern_proj")
        lo0_done, y1_last = sem("lo0_done"), sem("y1_last")
        proj_full, proj_copied = sem("proj_full"), sem("proj_copied")
        zeroed, pm_full, blk_done = sem("zeroed"), sem("pm_full"), sem("blk_done")
        gT_done, g_T = sem("gT_done"), sem("g_T")
        g_mm, g_done, m_full, m_done = sem("g_mm"), sem("g_done"), sem("m_full"), sem("m_done")
        e_in, e_out, prob0 = sem("e_in"), sem("e_out"), sem("prob0")
        f_fac, f_fc, f_gelu, f_norm, f_y, f_T, f_hi, f_lo, f_out, f_add = (
            sem("f_" + n) for n in ("fac", "fc", "gelu", "norm", "y", "T", "hi", "lo", "out", "add"))
        sh_full, sh_hi, sh_done = sem("sh_full"), sem("sh_hi"), sem("sh_done")
        full = {6: sem("full6"), 7: sem("full7")}
        free = {6: sem("free6"), 7: sem("free7")}
        k_products = sem("k_products")
        qn_done, kn_done = sem("qn_done"), sem("kn_done")
        s_full, s_max, s_exp, t_full, t_hi, t_lo, pv_done = (sem(n) for n in
                                                             ("s_full", "s_max", "s_exp", "t_full", "t_hi", "t_lo", "pv_done"))
        v_hi, rs_done, s_norm, o_hi, o_done = sem("v_hi"), sem("rs_done"), sem("s_norm"), sem("o_hi"), sem("o_done")
        stored = sem("stored")
        block = ctx.enter_context(nc.Block())

        FILLS = {7: ["q0", "kv", "qT0", "kT", "wo0", "qT2"], 6: ["q1", "qT1", "wo1", "qT3"]}
        PROJECT_UNITS = {0: "q0", 1: "kv", 2: "q1"}
        TURN_UNITS = {3: ("qT0", "qT1"), 4: ("kT",), 5: ("qT2", "qT3")}
        BEFORE, FIRST, INNER, LAST, AFTER = range(5)

        def present(b, kind):
            return [w for w in FILLS[b] if (w[0:2] == "wo" and kind in (INNER, LAST, AFTER))
                    or (w[0] in "qk" and kind in (BEFORE, FIRST, INNER))]

        def fills(b, it):
            return (it - 1) * len(FILLS[b]) + 2 * len(present(b, BEFORE))

        def place(what, it, kind):
            b = 7 if what in FILLS[7] else 6
            before = {BEFORE: 0, FIRST: len(present(b, BEFORE)), LAST: fills(b, ITS - 1), AFTER: fills(b, ITS - 1) + 1}
            return b, (before[kind] if kind in before else fills(b, it)) + present(b, kind).index(what)

        def iterations(engine, iteration):
            iteration(0, 0, FIRST)
            with engine.Fori(0, (ITS - B) // B) as i:
                for n in range(1, B + 1):
                    iteration(i * B + n, n % B, INNER)
            for n in (ITS - 3, ITS - 2, ITS - 1):
                iteration(n, n % B, LAST if n == ITS - 1 else INNER)

        def unit_heads(u):
            return (4, 4 * u, P) if u < 2 else (2, 2 * (u - 2), 2 * P)

        def head_places(u, par):
            heads, h, _ = unit_heads(u)
            c = 1 if u >= 2 else 0
            for odd in range(2):
                rows = slice(DH * odd, DH * odd + DH)
                yield (bank[4 + u % 2][rows, 0:P * heads].rearrange("p (j s q) -> p j s q", s=2, q=P)[:, :, odd, :],
                       *(oT[par][w][rows, h // 2:(h + heads) // 2, P * c:P * c + P] for w in range(2)))

        TILES = 8
        ALONE = 5
        STEPS = TILES + 4
        SHADE = [("qkvT", j) for j in range(RING_QKV, QKV1 // 256)] + [("woT", j) for j in range(HC // 2)]
        SHADE_EARLY = {2: (4,), 3: (7,), 4: (10,), 5: (13, 14)}
        SHADE_LATE = {0: (0, 1), 1: (2, 3), 2: (5, 6), 3: (8, 9), 4: (11, 12)}
        PREPARE_STEPS = {5: [("q0", -1), ("q1", -1)], 6: [("kv", -1)], 8: [("qT0", -1), ("qT1", -1)], 9: [("kT", -1)],
                         10: [("qT2", -1), ("qT3", -1)], 11: [("q0", 0), ("q1", 0)]}

        def hidden_bank(t, half):
            return bank[2 if half and t >= ALONE else 4]

        def shade_places(n):
            what, j = SHADE[n]
            src = bank[6 + n % 2][:, :].rearrange("p (k n) -> p k n", k=2)
            if what == "qkvT":
                return [w[:, :, 256 * j:256 * j + 256] for w in qkvT], src
            return [w[:, 2 * j:2 * j + 2, :] for w in woT], src

        def norm1(engine, b):
            for t in (2 * b, 2 * b + 1):
                ins = engine.tensor_scalar(y1[:, b, t % 2, :], x[:, b, t % 2, :], mv[:, t, 0:1], tok[:, 0, t:t + 1],
                                           ALU.subtract, ALU.mult)
            return ins

        @block.sync
        def _(sp):
            sp.dma_start(cst[:, 0:C_QC], const[:, 0:C_QC]).then_inc(ld["cst"], 16)
            for w in range(2):
                for d in range(2):
                    sp.dma_start(pmn[:, w, :, d, :], pm[w, :, 0:2, :]).then_inc(ld["pm"], 16)
            wq0_cols = w_qkv0.rearrange("(c p) n -> p c n", p=P)
            piece = H * DH // WQ0_PIECES
            for i in range(WQ0_PIECES):
                sp.dma_start(wq0[:, :, piece * i:piece * i + piece],
                             wq0_cols[:, :, piece * i:piece * i + piece]).then_inc(ld_wq0[i], 16)
                if i == 0:
                    sp.dma_start(x[:, :, :, :], seq.rearrange("b (p e) d -> p b e d", e=2)).then_inc(ld["x"], 16)
            sp.dma_start(nat_ffn0[:, :, :], w_ffn0.rearrange("(c p) i -> p c i", p=P)).then_inc(ld["ffn0"], 16)
            sp.dma_start(nat_fc[:, :, :], w_fc.rearrange("(c p) n -> p c n", p=P)).then_inc(ld["fc"], 16)
            sp.dma_start(nat_proj[:, :, :], w_proj.rearrange("(c p) n -> p c n", p=P)).then_inc(ld["proj"], 16)
            sp.dma_start(wout0[:, :, :], w_out0.rearrange("(c p) n -> p c n", p=P)).then_inc(ld["wout"], 16)
            sp.dma_start(nat_qkv[:, :, :], w_qkv1.rearrange("(c p) n -> p c n", p=P)).then_inc(ld["qkv"], 16)
            sp.dma_start(cst[:, C_QC:C_ALL], const[:, C_QC:C_ALL]).then_inc(ld["rope"], 16)
            sp.wait_ge(filled, UNIT[("out0", B - 1)] + 1)
            sp.dma_start(nat_o[:, :, :], w_o1.rearrange("(c p) n -> p c n", p=P)).then_inc(ld["o"], 16)
            rows = out.rearrange("b (p e) d -> p b e d", e=2)
            for it, kind, done in ((ITS - 1, LAST, slice(0, B - 1)), (ITS, AFTER, slice(B - 1, B))):
                for b, w in ((7, "wo0"), (6, "wo1")):
                    sp.wait_ge(free[b], place(w, it, kind)[1] + 1)
                sp.dma_start(rows[:, done, :, :], x[:, done, :, :]).then_inc(stored, 16)
            sp.wait_ge(stored, 32)

        @block.scalar
        def _(act):
            act.dma_start(vecs[:, :, :], vec).then_inc(ld["vec"], 16)
            act.dma_start(m0[2 * H:2 * H + 1, :], bias0.rearrange("(a n) -> a n", a=1)).then_inc(ld["bias"], 16)

            def unit(what, j=0):
                n = UNIT[(what, j)]
                act.wait_ge(filled, n + 1)
                return bank[n % RING]

            act.wait_ge(zeroed, 3)
            act.wait_ge(pm_full, 1)
            ps = bank[6][:, 0:4 * H].rearrange("p (w j c s) -> p w s c j", w=2, j=2, s=2)
            for w, blk in enumerate((blk_k, blk_v)):
                own = blk[:, :].rearrange("p (c n) -> p c n", n=68)
                for s in range(2):
                    rows = slice(DH * s, DH * s + DH)
                    ins = nc.scalar.activation(own[rows, :, 2 * s:2 * s + 2], ps[rows, w, s, :, :], ACT.Copy)
            ins.then_inc(blk_done, 1)
            for j in range(HC // 2):
                ps = unit("wq0T", j)
                if j >= 4:
                    act.wait_ge(g_mm, j - 3)
                nc.scalar.activation(wq0T[:, j % 4, :], ps[:, :], ACT.Copy).then_inc(rel["act"], 1)

            act.wait_ge(ld["vec"], 16)
            for b in range(B):
                ps = unit("yT0", b)[:, :].rearrange("p (k t) -> p k t", k=KC)
                for k in range(KC):
                    ins = nc.scalar.activation(yT_full[:, b, 256 * k:256 * k + 256], ps[:, k, :], ACT.Identity,
                                               bias=vecs[:, 1, k:k + 1], scale=vecs[:, 0, k:k + 1])
                ins.then_inc(full_done, 1)
                for k in range(KC):
                    ins = nc.scalar.activation(xrT[:, k, P * b:P * b + P], ps[:, k, P:2 * P], ACT.Identity,
                                               scale=vecs[:, 2, k:k + 1])
                ins.then_inc(rel["act"], 1)
            ps = unit("ffn0T")
            act.wait_ge(const_done, 1)
            nc.scalar.activation(ffn0T[:, :, :], ps[:, :].rearrange("p (k n) -> p k n", k=KC),
                                 ACT.Identity, bias=neg_magic[:, 0:1]).then_inc(rel["act"], 1)
            def fc_T(j):
                ps = unit("fcT", j)
                nc.scalar.activation(fcT[:, :, 256 * j:256 * j + 256], ps[:, :].rearrange("p (k n) -> p k n", k=KC),
                                     ACT.Identity, bias=neg_magic[:, 0:1]).then_inc(rel["act"], 1)

            act.wait_ge(e_in, 1)
            nc.scalar.activation(small[:, 1, :], small[:, 0, :], ACT.Exp).then_inc(e_out, 1)
            fc_T(0)
            fc_T(1)

            def qkv_hi(j):
                ps = unit("qkvT", j)
                nc.scalar.activation(qkvT[0][:, :, 256 * j:256 * j + 256], ps[:, :].rearrange("p (k n) -> p k n", k=KC),
                                     ACT.Copy).then_inc(hi_done, 1)

            def y1_hi(b):
                ps = unit("yT1", b)[:, :].rearrange("p (k e t) -> p k t e", k=KC, e=2)
                for k in range(KC):
                    ins = nc.scalar.activation(xT[0][:, k, SEQ * b:SEQ * b + SEQ].rearrange("p (t e) -> p t e", e=2),
                                               ps[:, k, :, :], ACT.Copy)
                ins.then_inc(hi_done, 1)

            for what, j in ORDER[UNIT[("fcT", 2)]:UNIT[("yT1", 2)]]:
                if what == "fcT":
                    fc_T(j)
                elif what == "probT0":
                    ps = unit("probT0")
                    nc.scalar.activation(probT0[0:2 * H, :], ps[0:2 * H, :], ACT.Copy).then_inc(rel["act"], 1)
                elif what == "qkvT":
                    qkv_hi(j)
                elif what == "yT1":
                    y1_hi(j)

            def copy_q(c, it, kind):
                b, n = place(f"q{c}", it, kind)
                act.wait_ge(full[b], n + 1)
                if kind != BEFORE:
                    act.wait_ge(qn_done, it * 2 + c + 1)
                nc.scalar.activation(q_raw[:, c, :], bank[b][:, :], ACT.Copy).then_inc(free[b], 1)

            def hi_lo_T(what, it, kind, par):
                b, n = place(what, it, kind)
                act.wait_ge(full[b], n + 1)
                if what == "kT":
                    dst = kT[par][:, :, :]
                    src = bank[b][:, :].rearrange("p (s t) -> p s t", s=2)
                else:
                    j = int(what[2])
                    c, h = j // 2, 4 * (j % 2)
                    dst = qT[par][:, h:h + 4, P * c:P * c + P]
                    src = bank[b][:, :].rearrange("p (h t) -> p h t", h=4)
                nc.scalar.activation(dst, src, ACT.Copy).then_inc(free[b], 1)

            def gelu(t):
                act.wait_ge(f_fc, t + 1)
                for half in range(2):
                    ins = nc.scalar.activation(ffn_h[t][:, 512 * half:512 * half + 512],
                                               bank[2 * (t % 2) + half][:, :], ACT.Gelu, scale=ffac[:, t, 0:1])
                ins.then_inc(f_gelu, 1)

            def hidden_hi(t, half):
                if 0 <= t < TILES:
                    act.wait_ge(f_T, 2 * t + half + 1)
                    nc.scalar.activation(hT[t % 2][0][:, 4 * half:4 * half + 4, :],
                                         hidden_bank(t, half)[:, :].rearrange("p (k n) -> p k n", k=4),
                                         ACT.Copy).then_inc(f_hi, 1)

            def hidden_y(t):
                act.wait_ge(f_norm, t + 1)
                nc.scalar.activation(ffn_h[t][:, :], ffn_h[t][:, :], ACT.Identity, bias=ffac[:, t, 4:5],
                                     scale=ffac[:, t, 3:4]).then_inc(f_y, 1)

            def proj_hi(j):
                act.wait_ge(proj_full, j + 1)
                nc.scalar.activation(projT[:, 2 * j:2 * j + 2, :], bank[4 + j % 2][:, :].rearrange("p (k n) -> p k n", k=2),
                                     ACT.Identity, bias=neg_magic[:, 0:1]).then_inc(proj_copied, 1)

            def shade_hi(units):
                for n in units:
                    act.wait_ge(sh_full, n + 1)
                    (hi, _), src = shade_places(n)
                    nc.scalar.activation(hi, src, ACT.Copy).then_inc(sh_hi, 1)

            def prepared(step):
                for what, it in PREPARE_STEPS.get(step, ()):
                    if what in ("q0", "q1"):
                        copy_q(int(what[1]), it, FIRST if it == 0 else BEFORE)
                    elif what != "kv":
                        hi_lo_T(what, it, BEFORE, 0)

            nc.scalar.activation(table_use[:, 0:1], neg_magic[:, :], ACT.Gelu)
            act.wait_ge(f_fac, 1)
            for step in range(STEPS):
                hidden_hi(step - 3, 0)
                if 0 <= step - 2 < TILES:
                    hidden_y(step - 2)
                prepared(step - 1)
                shade_hi(SHADE_EARLY.get(step, ()))
                if step == 2:
                    proj_hi(0)
                    proj_hi(1)
                hidden_hi(step - 3, 1)
                if step < TILES:
                    gelu(step)
                if step == 1:
                    y1_hi(2)
                    y1_hi(3)
                if step == 2:
                    proj_hi(2)
                    proj_hi(3)
                shade_hi(SHADE_LATE.get(step, ()))

            def probs(it, u, par, kind):
                n = it * UNITS + u
                if u >= 3 or kind != FIRST:
                    act.wait_ge(t_full, n - 2)
                act.wait_ge(s_max, n + 1)
                heads, h, wide = unit_heads(u)
                h += 8 * (u >= 2)
                for j in range(heads):
                    ins = nc.scalar.activation(prob[u % 3][:, wide * j:wide * j + wide], bank[u % 2][:, wide * j:wide * j + wide],
                                               ACT.Exp, bias=neg_max[par][:, h + j:h + j + 1],
                                               accum_out=sums[par][:, h + j:h + j + 1])
                ins.then_inc(s_exp, 1)

            def probs_T(it, u, early=False):
                n = it * UNITS + u
                act.wait_ge(t_full, n + 1)
                if not early:
                    act.wait_ge(pv_done, n - 1)
                nc.scalar.activation(probT[u % 2][0][:, :], bank[2 + u % 2][:, :], ACT.Copy).then_inc(t_hi, 1)

            def heads_hi(it, u, par, first=False):
                act.wait_ge(pv_done, it * UNITS + u + 1)
                if u == 0 and not first:
                    for b in (6, 7):
                        act.wait_ge(full[b], fills(b, it))
                for src, hi, _ in head_places(u, par):
                    ins = nc.scalar.activation(hi, src, ACT.Copy)
                ins.then_inc(o_hi, 1)

            def iteration(it, b_it, kind):
                par = b_it % 2
                for u in range(UNITS):
                    if u >= 2:
                        probs_T(it, u - 2, early=kind == FIRST and u < 4)
                    elif kind != FIRST:
                        probs_T(it - 1, u + 4)
                    if u in (0, 2) and kind == INNER:
                        copy_q(u // 2, it, kind)
                    if u >= 3:
                        heads_hi(it, u - 3, par, first=kind == FIRST)
                    elif kind != FIRST:
                        heads_hi(it - 1, u + 3, 1 - par)
                    probs(it, u, par, kind)
                    if kind != LAST:
                        for what in TURN_UNITS.get(u, ()):
                            hi_lo_T(what, it, kind, 1 - par)

            prepared(STEPS - 1)
            nc.scalar.activation(table_use[:, 1:2], neg_magic[:, :], ACT.Exp)
            iterations(act, iteration)
            for u in (4, 5):
                probs_T(ITS - 1, u)
                heads_hi(ITS - 1, u - 1, 1)
            heads_hi(ITS - 1, 5, 1)

        @block.gpsimd
        def _(pool):
            pool.memset(blk_k[:, :], 0.0).then_inc(zeroed, 1)
            pool.memset(blk_v[:, :], 0.0).then_inc(zeroed, 1)
            pool.wait_ge(zeroed, 2)
            pool.memset(probT0[2 * H:2 * H + 1, :], 1.0).then_inc(zeroed, 1)
            pool.wait_ge(zeroed, 3)
            pool.memset(neg_half[:, :, :], -0.5).then_inc(zeroed, 1)
            pool.wait_ge(zeroed, 4)

            def root(a, n):
                pool.wait_ge(root_in, n)
                pool.tensor_tensor(a, a, neg_half[:, 0:a.shape[1], 0:a.shape[2]], ALU.pow).then_inc(root_out, 1)

            def own(ins, n):
                ins.then_inc(s_pool, 1)
                pool.wait_ge(s_pool, n)

            root(tok[:, 0:1, :], 1)
            root(tok[:, 4:5, :], 2)
            for b in range(B):
                root(tok[:, 0:2, 2 * b:2 * b + 2], b + 3)
            pool.wait_ge(root_out, B + 2)
            norm1(pool, B - 1).then_inc(y1_last, 1)
            OWN = 5

            def rope_views(c):
                return (t[:, c, :].rearrange("p (h d) -> p h d", h=HG) for t in (q_raw, rope_a, rope_b))

            def rope_products(c, it, kind, n):
                b, m = place(f"q{c}", it, kind)
                pool.wait_ge(free[b], m + 1)
                q, a, z = rope_views(c)
                cos = cst[:, C_QC + DH * c:C_QC + DH * c + DH].rearrange("p (a n) -> p a n", a=1).to_broadcast([P, HG, DH])
                sin = cst[:, C_QS + DH * c:C_QS + DH * c + DH].rearrange("p (a n) -> p a n", a=1)
                half = DH // 2
                pool.tensor_tensor(a, q, cos, ALU.mult)
                for s in range(2):
                    dst, src = slice(half * s, half * s + half), slice(half * (1 - s), half * (1 - s) + half)
                    ins = pool.tensor_tensor(z[:, :, dst], q[:, :, src], sin[:, :, dst].to_broadcast([P, HG, half]), ALU.mult)
                own(ins, n + 3 * c + 1)

            def rope_sums(c, it, kind, n):
                if kind != BEFORE:
                    for b in (6, 7):
                        pool.wait_ge(full[b], (len(present(b, BEFORE)) if kind == FIRST else fills(b, it)) - 1 + c)
                _, a, z = rope_views(c)
                hi, lo = (q_nat[:, c, :, s, :] for s in range(2))
                pool.tensor_tensor(hi.bitcast(F32R), a, z, ALU.add)
                own(pool.tensor_tensor(a, a, z, ALU.add), n + 3 * c + 2)
                pool.tensor_tensor(lo, a, hi, ALU.subtract).then_inc(qn_done, 1)

            def keys(it, kind, n):
                pool.wait_ge(k_products, it + 2)
                k1, k2 = rope_k[:, 0, :, :], rope_k[:, 1, :, :]
                twice1, twice2 = (rope_k[:, w, :, :].rearrange("p c (w d) -> p c w d", w=1).to_broadcast([P, 2, 2, DH])
                                  for w in range(2))
                pool.tensor_tensor(k_nat[:, 0, :, :, :].bitcast(F32R), twice1, twice2, ALU.add)
                own(pool.tensor_tensor(k_sum[:, :, :], k1, k2, ALU.add), n + 3)
                total = k_sum[:, :, :].rearrange("p c (w d) -> p c w d", w=1).to_broadcast([P, 2, 2, DH])
                pool.tensor_tensor(k_nat[:, 1, :, :, :], total, k_nat[:, 0, :, :, :], ALU.subtract).then_inc(kn_done, 1)

            def prepare(it, kind, n):
                rope_products(0, it, kind, n)
                rope_sums(0, it, kind, n)
                keys(it, kind, n)
                rope_products(1, it, kind, n)
                rope_sums(1, it, kind, n)

            def tile_root(t):
                root(ffac[:, t:t + 1, 1:2], t + B + 3)

            for t in range(TILES - 2):
                tile_root(t)
            pool.wait_ge(ld["rope"], 16)
            rope_products(0, -1, BEFORE, 0)
            tile_root(TILES - 2)
            rope_sums(0, -1, BEFORE, 0)
            keys(-1, BEFORE, 0)
            tile_root(TILES - 1)
            rope_products(1, -1, BEFORE, 0)
            rope_sums(1, -1, BEFORE, 0)
            prepare(0, FIRST, OWN)
            with pool.Fori(1, ITS - 2) as it:
                prepare(it, INNER, OWN * (it + 1))
            prepare(ITS - 2, INNER, OWN * (ITS - 1))

        @block.vector
        def _(dve):
            count = [0]

            def link(ins):
                count[0] += 1
                ins.then_inc(s_dve, 1)
                dve.wait_ge(s_dve, count[0])

            def ask(dst, src, eps):
                dve.tensor_scalar(dst, src, eps, None, ALU.add).then_inc(root_in, 1)

            def unit(what, j=0):
                n = UNIT[(what, j)]
                dve.wait_ge(filled, n + 1)
                return bank[n % RING]

            def layer_stats(tiles):
                for t in tiles:
                    ins = dve.bn_stats(stats[:, t, :], x[:, t // 2, t % 2, :])
                link(ins)
                for t in tiles:
                    ins = dve.bn_aggr(mv[:, t, :], stats[:, t, :])
                link(ins)

            r, c, ms, rc, f1 = (tok[:, i, :] for i in (0, 1, 2, 0, 4))
            mean, var = mv[:, :, 0], mv[:, :, 1]

            dve.memset(neg_magic[:, :], -MAGIC)
            dve.wait_ge(ld["cst"], 16)
            dve.tensor_copy(ident_b[:, :], ident)
            for j in range(4):
                ins = dve.tensor_copy(mask_b[:, j, :], cst[:, C_MASK:C_MASK + P])
            ins.then_inc(const_done, 1)
            dve.wait_ge(ld["x"], 16)
            layer_stats(range(8))
            dve.tensor_scalar(rc, var, 1.0 + EPS_LN, EPS_LN * EPS_LN, ALU.mult, ALU.add).then_inc(root_in, 1)
            link(dve.tensor_scalar(ms, var, EPS_LN, None, ALU.add))
            link(dve.reciprocal(ms, ms))
            link(dve.tensor_tensor(ms, ms, var, ALU.mult))
            link(dve.tensor_scalar(c, ms, EPS_LN, None, ALU.add))
            link(dve.reciprocal(c, c))
            link(dve.tensor_scalar(ms, ms, EPS_RMS, None, ALU.add))
            dve.tensor_tensor(f1, ms, c, ALU.mult).then_inc(root_in, 1)
            for n, (name, w) in enumerate((("ffn0", nat_ffn0), ("fc", nat_fc))):
                dve.wait_ge(ld[name], 16)
                ins = dve.tensor_reduce(wsum[:, n:n + 1], w[:, :, :], AX.XY, ALU.add, apply_absolute_value=True)
            ins.then_inc(sum_in, 1)
            dve.wait_ge(root_out, 1)
            for t in range(8):
                ins = dve.tensor_scalar(y0[:, t // 2, t % 2, :], x[:, t // 2, t % 2, :], mean[:, t:t + 1], rc[:, t:t + 1],
                                        ALU.subtract, ALU.mult)
                if t % 2:
                    ins.then_inc(y0_done, 1)

            def ternary(w, inverse):
                link(dve.tensor_scalar(w, w, inverse, 1.0, ALU.mult, ALU.min))
                return dve.tensor_scalar(w, w, -1.0, MAGIC, ALU.max, ALU.add)

            dve.wait_ge(g_mm, HC // 2)
            dve.tensor_copy(gT[:, :], bank[6][0:2 * H, 0:DIM]).then_inc(gT_done, 1)
            dve.wait_ge(sum_out, 1)
            dve.tensor_scalar(winv[:, 0:1], bank[7][:, 0:1], 1.0 / (DIM * DIM), 1e-5, ALU.mult, ALU.add)
            link(dve.tensor_scalar(wscale[:, 1:2], bank[7][:, 1:2], 1.0 / (DIM * FF), None, ALU.mult))
            link(dve.tensor_scalar(winv[:, 1:2], wscale[:, 1:2], EPS_BIT, None, ALU.add))
            link(dve.reciprocal(winv[:, 0:2], winv[:, 0:2]))
            dve.wait_ge(g_T, 1)
            dve.tensor_copy(g0[:, :, :], bank[7][:, P:2 * P].rearrange("p (k n) -> p k n", k=KC)).then_inc(g_done, 1)
            ternary(nat_ffn0[:, :, :], winv[:, 0:1]).then_inc(tern0, 1)
            def split_yT(b):
                dve.wait_ge(full_done, b + 1)
                at = slice(SEQ * b, SEQ * b + SEQ)
                whole = yT_full[:, b, :].rearrange("p (k t) -> p k t", k=KC)
                dve.tensor_copy(xT[0][:, :, at], whole).then_inc(x_hi, 1)
                dve.wait_ge(x_hi, b + 1)
                dve.tensor_tensor(xT[1][:, :, at], whole, xT[0][:, :, at].bitcast(F32), ALU.subtract).then_inc(lo0_done, 1)

            split_yT(0)
            split_yT(1)
            ps = unit("score0")
            dve.wait_ge(root_out, 2)
            for b in range(B):
                at = slice(2 * H * b, 2 * H * b + 2 * H)
                ins = dve.tensor_scalar(small[:, 3, at], ps[:, at], f1[:, 2 * b + 1:2 * b + 2], DH ** -0.5, ALU.mult, ALU.mult)
            ins.then_inc(rel["dve"], 1)
            dve.wait_ge(rel["dve"], released("dve", UNIT[("score0", 0)]))
            pair = small[:, :, :].rearrange("p w (n j) -> p w n j", j=2)
            top = small[:, 2, 0:H * B]
            link(dve.tensor_tensor(top, pair[:, 3, :, 0], pair[:, 3, :, 1], ALU.max))
            for j in range(2):
                ins = dve.tensor_tensor(pair[:, 0, :, j], pair[:, 3, :, j], top, ALU.subtract)
            ins.then_inc(e_in, 1)
            ternary(nat_fc[:, :, :], winv[:, 1:2]).then_inc(tern_fc, 1)
            dve.wait_ge(e_out, 1)
            link(dve.tensor_tensor(top, pair[:, 1, :, 0], pair[:, 1, :, 1], ALU.add))
            link(dve.reciprocal(top, top))
            for j in range(2):
                ins = dve.tensor_tensor(pair[:, 3, :, j], pair[:, 1, :, j], top, ALU.mult)
            ins.then_inc(prob0, 1)
            split_yT(2)
            split_yT(3)
            dve.wait_ge(ld["proj"], 16)
            dve.tensor_reduce(wsum[:, 2:3], nat_proj[:, :, :], AX.XY, ALU.add, apply_absolute_value=True).then_inc(sum_in, 1)
            dve.wait_ge(m_full, 1)
            dve.tensor_copy(m0[0:2 * H, :], bank[6][0:2 * H, 0:DIM]).then_inc(m_done, 1)
            dve.wait_ge(sum_out, 2)
            link(dve.tensor_scalar(wscale[:, 2:3], bank[7][:, 2:3], 1.0 / (DIM * FF), None, ALU.mult))
            link(dve.tensor_scalar(winv[:, 2:3], wscale[:, 2:3], EPS_BIT, None, ALU.add))
            link(dve.reciprocal(winv[:, 2:3], winv[:, 2:3]))

            def qkv_lo(j):
                ps = unit("qkvT", j)
                at = slice(256 * j, 256 * j + 256)
                dve.wait_ge(hi_done, HI[("qkvT", j)])
                dve.tensor_tensor(qkvT[1][:, :, at], ps[:, :].rearrange("p (k n) -> p k n", k=KC),
                                  qkvT[0][:, :, at].bitcast(F32), ALU.subtract).then_inc(rel["dve"], 1)

            def y1_lo(b):
                ps = unit("yT1", b)[:, :].rearrange("p (k e t) -> p k t e", k=KC, e=2)
                dve.wait_ge(hi_done, HI[("yT1", b)])
                for k in range(KC):
                    at = slice(SEQ * b, SEQ * b + SEQ)
                    ins = dve.tensor_tensor(xT[1][:, k, at].rearrange("p (t e) -> p t e", e=2), ps[:, k, :, :],
                                            xT[0][:, k, at].bitcast(F32).rearrange("p (t e) -> p t e", e=2), ALU.subtract)
                ins.then_inc(rel["dve"], 1)

            for j in range(2):
                qkv_lo(j)

            for what, b in ORDER[UNIT[("out0", 0)]:UNIT[("yT1", 2)]]:
                if what == "qkvT":
                    qkv_lo(b)
                elif what == "yT1":
                    y1_lo(b)
                else:
                    ps = unit("out0", b)
                    dve.tensor_tensor(x[:, b, :, :], x[:, b, :, :], ps[:, :].rearrange("p (e n) -> p e n", e=2),
                                      ALU.add).then_inc(rel["dve"], 1)
                    dve.wait_ge(rel["dve"], released("dve", UNIT[("out0", b)]))
                    layer_stats((2 * b, 2 * b + 1))
                    own = slice(2 * b, 2 * b + 2)
                    link(dve.tensor_scalar(r[:, own], var[:, own], EPS_LN, None, ALU.add))
                    link(dve.reciprocal(ms[:, own], r[:, own]))
                    link(dve.tensor_tensor(ms[:, own], ms[:, own], var[:, own], ALU.mult))
                    ask(c[:, own], ms[:, own], EPS_BIT)
                    if b >= 1:
                        dve.wait_ge(root_out, b + 2)
                        norm1(dve, b - 1).then_inc(y1_done, 1)
            dve.wait_ge(root_out, B + 2)
            link(dve.reciprocal(f1, ms))
            link(dve.tensor_tensor(f1, f1, ms, ALU.mult))
            link(dve.tensor_tensor(c, c, f1, ALU.mult))
            dve.tensor_scalar(ffac[:, :, 0], c, wscale[:, 1:2], None, ALU.mult).then_inc(f_fac, 1)

            def hidden_stats(t):
                dve.wait_ge(f_gelu, t + 1)
                dve.bn_stats(fstat[:, t, 0:6], ffn_h[t][:, 0:512])
                link(dve.bn_stats(fstat[:, t, 6:12], ffn_h[t][:, 512:1024]))
                link(dve.bn_aggr(fmv[:, t, :], fstat[:, t, :]))
                fm, fv = fmv[:, t, 0:1], fmv[:, t, 1:2]
                ask(ffac[:, t, 1:2], fv, EPS_BIT)
                link(dve.reciprocal(ffac[:, t, 2:3], fv))
                link(dve.tensor_tensor(ffac[:, t, 2:3], ffac[:, t, 2:3], fv, ALU.mult))

            def hidden_factors(t):
                dve.wait_ge(root_out, t + B + 3)
                link(dve.tensor_scalar(ffac[:, t, 3:4], ffac[:, t, 1:2], ffac[:, t, 2:3], wscale[:, 2:3], ALU.mult, ALU.mult))
                dve.tensor_scalar(ffac[:, t, 4:5], ffac[:, t, 3:4], fmv[:, t, 0:1], -1.0, ALU.mult, ALU.mult).then_inc(f_norm, 1)

            def hidden_lo(t, half):
                dve.wait_ge(f_hi, 2 * t + half + 1)
                dve.tensor_tensor(hT[t % 2][1][:, 4 * half:4 * half + 4, :], hidden_bank(t, half)[:, :].rearrange("p (k n) -> p k n", k=4),
                                  hT[t % 2][0][:, 4 * half:4 * half + 4, :].bitcast(F32), ALU.subtract).then_inc(f_lo, 1)

            def ffn_add(t):
                dve.wait_ge(f_out, t + 1)
                dve.tensor_tensor(x[:, t // 2, t % 2, :], x[:, t // 2, t % 2, :], bank[5][:, 0:DIM],
                                  ALU.add).then_inc(f_add, 1)

            def rope_k_products(it, kind):
                b, n = place("kv", it, kind)
                dve.wait_ge(full[b], n + 1)
                if kind != BEFORE:
                    dve.wait_ge(kn_done, it + 1)
                kv = bank[b][:, 0:2 * P].rearrange("p (c w d) -> p c w d", c=2, w=2)
                cos = cst[:, C_KC:C_KC + P].rearrange("p (c d) -> p c d", c=2)
                sin = cst[:, C_KS:C_KS + P].rearrange("p (c s d) -> p c s d", c=2, s=2)
                dve.tensor_tensor(rope_k[:, 0, :, :], kv[:, :, 0, :], cos, ALU.mult)
                for s in range(2):
                    d = DH // 2
                    ins = dve.tensor_tensor(rope_k[:, 1, :, d * s:d * s + d], kv[:, :, 0, d * (1 - s):d * (1 - s) + d],
                                            sin[:, :, s, :], ALU.mult)
                ins.then_inc(k_products, 1)

            def values(it, kind, par):
                b, n = place("kv", it, kind)
                if kind not in (BEFORE, FIRST):
                    dve.wait_ge(pv_done, it * UNITS)
                kv = bank[b][:, 0:2 * P].rearrange("p (c w d) -> p c w d", c=2, w=2)
                val = kv[:, :, 1, :].rearrange("p c (a d) -> p c a d", a=1).to_broadcast([P, 2, 2, DH])
                hi, lo = (v[par][:, :, s, :].rearrange("p c (t d) -> p c t d", t=2) for s in range(2))
                dve.tensor_copy(hi, val).then_inc(v_hi, 1)
                dve.wait_ge(v_hi, it + 2)
                dve.tensor_tensor(lo, val, hi.bitcast(F32), ALU.subtract).then_inc(free[b], 1)

            def shade_lo(units):
                for n in units:
                    dve.wait_ge(sh_hi, n + 1)
                    (hi, lo), src = shade_places(n)
                    dve.tensor_tensor(lo, src, hi.bitcast(F32), ALU.subtract).then_inc(sh_done, 1)

            for step in range(STEPS):
                t = step - 3
                if 0 <= t < TILES:
                    hidden_lo(t, 0)
                if 1 <= step <= TILES:
                    hidden_stats(step - 1)
                if step == 0:
                    ternary(nat_proj[:, :, :], winv[:, 2:3]).then_inc(tern_proj, 1)
                if step == 1:
                    y1_lo(2)
                    y1_lo(3)
                shade_lo(SHADE_EARLY.get(step, ()))
                if ("kv", -1) in PREPARE_STEPS.get(step - 1, ()):
                    dve.wait_ge(ld["rope"], 16)
                    rope_k_products(-1, BEFORE)
                    values(-1, BEFORE, 0)
                if 0 <= t < TILES:
                    hidden_lo(t, 1)
                if 1 <= step <= TILES:
                    hidden_factors(step - 1)
                if t >= 1:
                    ffn_add(t - 1)
                shade_lo(SHADE_LATE.get(step, ()))

            def maxima(it, u, par):
                dve.wait_ge(s_full, it * UNITS + u + 1)
                heads, h, _ = unit_heads(u)
                h += 8 * (u >= 2)
                dve.tensor_reduce(neg_max[par][:, h:h + heads], bank[u % 2][:, :].rearrange("p (h k) -> p h k", h=heads),
                                  AX.X, ALU.max, negate=True).then_inc(s_max, 1)

            def probs_lo(it, u):
                dve.wait_ge(t_hi, it * UNITS + u + 1)
                hi, lo = probT[u % 2]
                dve.tensor_tensor(lo[:, :], bank[2 + u % 2][:, :], hi[:, :].bitcast(F32), ALU.subtract).then_inc(t_lo, 1)

            def normalise(it, u, par):
                n = it * UNITS + u
                dve.wait_ge(s_exp, n + 1)
                heads, h, wide = unit_heads(u)
                h += 8 * (u >= 2)
                dve.reciprocal(rsum[par][:, h:h + heads], sums[par][:, h:h + heads]).then_inc(rs_done, 1)
                dve.wait_ge(rs_done, n + 1)
                for j in range(heads):
                    a = prob[u % 3][:, wide * j:wide * j + wide]
                    ins = dve.tensor_scalar(a, a, rsum[par][:, h + j:h + j + 1], None, ALU.mult)
                ins.then_inc(s_norm, 1)

            def heads_lo(it, u, par):
                dve.wait_ge(o_hi, it * UNITS + u + 1)
                for src, hi, lo in head_places(u, par):
                    ins = dve.tensor_tensor(lo, src, hi.bitcast(F32), ALU.subtract)
                ins.then_inc(o_done, 1)

            def add_out(e, it, kind, b_last):
                b, n = place(f"wo{e}", it, kind)
                dve.wait_ge(full[b], n + 1)
                dst = x[:, b_last, e, :]
                dve.tensor_tensor(dst, dst, bank[b][:, 0:DIM], ALU.add).then_inc(free[b], 1)

            def iteration(it, b_it, kind):
                par = b_it % 2
                for u in range(UNITS):
                    maxima(it, u, par)
                    if u >= 1:
                        normalise(it, u - 1, par)
                    elif kind != FIRST:
                        normalise(it - 1, 5, 1 - par)
                    if u >= 2:
                        probs_lo(it, u - 2)
                    elif kind != FIRST:
                        probs_lo(it - 1, u + 4)
                    if u >= 3:
                        heads_lo(it, u - 3, par)
                    elif kind != FIRST:
                        heads_lo(it - 1, u + 3, 1 - par)
                    if u == 1 and kind != LAST:
                        rope_k_products(it, kind)
                    if u == 2 and kind != LAST:
                        values(it, kind, 1 - par)
                if kind != FIRST:
                    add_out(0, it, kind, (b_it - 1) % B)
                    add_out(1, it, kind, (b_it - 1) % B)

            iterations(dve, iteration)
            normalise(ITS - 1, 5, 1)
            for u in (4, 5):
                probs_lo(ITS - 1, u)
                heads_lo(ITS - 1, u - 1, 1)
            heads_lo(ITS - 1, 5, 1)
            for e in range(2):
                add_out(e, ITS, AFTER, B - 1)

        @block.tensor
        def _(pe):
            def ring(what, j=0):
                n = UNIT[(what, j)]
                if n >= RING:
                    engine = RELEASES[ORDER[n - RING][0]]
                    pe.wait_ge(rel[engine], released(engine, n - RING))
                return bank[n % RING]

            def transposes(ps, blocks):
                for j, a in enumerate(blocks):
                    ins = pe.transpose(ps[:, P * j:P * j + P], a, ident)
                return ins

            pe.wait_ge(ld["cst"], 16)
            ones = cst[:, C_ONE:C_ONE + P]
            pe.wait_ge(ld["pm"], 64)
            for w in range(2):
                for j in range(2):
                    col = (2 * w + j) * H
                    ins = pe.transpose(bank[6][:, col:col + H], pmn[:, w, j, :, :].rearrange("p a d -> p (a d)"), cst[0:H, C_ID:C_ID + H])
            ins.then_inc(pm_full, 1)

            def g_products(j):
                pe.wait_ge(rel["act"], released("act", UNIT[("wq0T", j)]))
                for c in (2 * j, 2 * j + 1):
                    ins = pe.matmul(bank[6][0:2 * H, 0:DIM], blk_k[:, 64 * c:64 * c + 64], wq0T[:, j % 4, DIM * (c % 2):DIM * (c % 2) + DIM],
                                    start=c == 0, stop=c == HC - 1)
                ins.then_inc(g_mm, 1)

            for j in range(HC // 2):
                if j % 2 == 0:
                    pe.wait_ge(ld_wq0[j // 2], 16)
                ps = ring("wq0T", j)
                transposes(ps, [wq0[:, k, P * c:P * c + P] for c in (2 * j, 2 * j + 1) for k in range(KC)]).then_inc(filled, 1)
                if j == 1:
                    pe.wait_ge(blk_done, 1)
                if j >= 1:
                    g_products(j - 1)
            g_products(HC // 2 - 1)

            for b in range(B):
                ps = ring("yT0", b)
                pe.wait_ge(y0_done, b + 1)
                transposes(ps, [y0[:, b, e, P * k:P * k + P] for k in range(KC) for e in range(2)]).then_inc(filled, 1)
            pe.wait_ge(gT_done, 1)
            for k in range(KC):
                ins = pe.transpose(bank[7][:, P + 2 * H * k:P + 2 * H * k + 2 * H], gT[:, P * k:P * k + P], cst[0:2 * H, C_ID:C_ID + 2 * H])
            ins.then_inc(g_T, 1)
            pe.wait_ge(sum_in, 1)
            pe.matmul(bank[7][:, 0:2], ones, wsum[:, 0:2], start=True, stop=True).then_inc(sum_out, 1)
            ps = ring("ffn0T")
            pe.wait_ge(tern0, 1)
            transposes(ps, [nat_ffn0[:, o, P * k:P * k + P] for k in range(KC) for o in range(2)]).then_inc(filled, 1)
            ps = ring("score0")
            pe.wait_ge(g_done, 1)
            pe.wait_ge(rel["act"], released("act", UNIT[("yT0", B - 1)]))
            for b in range(B):
                for k in range(KC):
                    ins = pe.matmul(ps[:, 2 * H * b:2 * H * b + 2 * H], xrT[:, k, P * b:P * b + P], g0[:, k, :],
                                    start=k == 0, stop=k == KC - 1)
            ins.then_inc(filled, 1)
            pe.wait_ge(ld["wout"], 16)
            for c in range(HC):
                ins = pe.matmul(bank[6][0:2 * H, 0:DIM], blk_v[:, 64 * c:64 * c + 64], wout0[:, c, :],
                                start=c == 0, stop=c == HC - 1)
            ins.then_inc(m_full, 1)

            def qkv_T(j):
                ps = ring("qkvT", j)
                transposes(ps, [nat_qkv[:, c, P * k:P * k + P] for k in range(KC) for c in (2 * j, 2 * j + 1)]).then_inc(filled, 1)

            for j in range(FF // 256):
                ps = ring("fcT", j)
                pe.wait_ge(tern_fc, 1)
                transposes(ps, [nat_fc[:, c, P * k:P * k + P] for k in range(KC) for c in (2 * j, 2 * j + 1)]).then_inc(filled, 1)
            pe.wait_ge(ld["qkv"], 16)
            qkv_T(0)
            pe.wait_ge(sum_in, 2)
            pe.matmul(bank[7][:, 2:3], ones, wsum[:, 2:3], start=True, stop=True).then_inc(sum_out, 1)
            ps = ring("probT0")
            pe.wait_ge(prob0, 1)
            for b in range(B):
                ins = pe.transpose(ps[0:2 * H, P * b:P * b + P], small[:, 3, 2 * H * b:2 * H * b + 2 * H], ident)
            ins.then_inc(filled, 1)
            qkv_T(1)

            pe.wait_ge(m_done, 1)
            pe.wait_ge(ld["bias"], 16)

            def out_0(b):
                ps = ring("out0", b)
                if b == 0:
                    pe.wait_ge(rel["act"], released("act", UNIT[("probT0", 0)]))
                pe.wait_ge(lo0_done, b + 1)
                for e in range(2):
                    o = ps[:, DIM * e:DIM * e + DIM]
                    p = probT0[:, P * b:P * b + P] if e else cst[0:2 * H + 1, C_EVEN:C_EVEN + P]
                    pe.matmul(o, p, m0[:, :], start=True, stop=False)
                    for k in range(KC):
                        for s in range(2):
                            col = SEQ * b + P * e
                            ins = pe.matmul(o, xT[s][:, k, col:col + P], ffn0T[:, k, :], start=False,
                                            stop=k == KC - 1 and s == 1)
                ins.then_inc(filled, 1)

            def y1_T(b):
                ps = ring("yT1", b)
                if b < B - 1:
                    pe.wait_ge(y1_done, b + 1)
                else:
                    pe.wait_ge(y1_last, 1)
                transposes(ps, [y1[:, b, e, P * k:P * k + P] for k in range(KC) for e in range(2)]).then_inc(filled, 1)

            for what, j in ORDER[UNIT[("out0", 0)]:UNIT[("yT1", 2)]]:
                if what == "out0":
                    out_0(j)
                elif what == "qkvT":
                    qkv_T(j)
                else:
                    y1_T(j)

            def fc(t):
                if t >= 2:
                    pe.wait_ge(f_gelu, t - 1)
                col = SEQ * (t // 2) + t % 2
                for half in range(2):
                    n = 0
                    for k in range(KC):
                        for s in range(2):
                            ins = pe.matmul(bank[2 * (t % 2) + half][:, :], xT[s][:, k, col:col + 2 * P - 1:2],
                                            fcT[:, k, 512 * half:512 * half + 512], start=n == 0, stop=n == 3)
                            n += 1
                ins.then_inc(f_fc, 1)

            def hidden_T(t, half):
                pe.wait_ge(f_y, t + 1)
                if t == ALONE and half == 1:
                    pe.wait_ge(f_gelu, TILES)
                elif t > ALONE:
                    pe.wait_ge(f_lo, 2 * t + half - 1)
                elif t or half:
                    pe.wait_ge(f_lo, 2 * t + half)
                transposes(hidden_bank(t, half), [ffn_h[t][:, P * k:P * k + P] for k in range(4 * half, 4 * half + 4)]).then_inc(f_T, 1)

            def proj(t):
                pe.wait_ge(f_lo, 2 * t + 2)
                if t >= 1:
                    pe.wait_ge(f_add, t)
                n = 0
                for k in range(FF // P):
                    for s in range(2):
                        ins = pe.matmul(bank[5][:, 0:DIM], hT[t % 2][s][:, k, :], projT[:, k, :],
                                        start=n == 0, stop=n == 2 * FF // P - 1)
                        n += 1
                ins.then_inc(f_out, 1)

            def shade_T(n):
                if n >= 2:
                    pe.wait_ge(sh_done, n - 1)
                what, j = SHADE[n]
                if what == "qkvT":
                    blocks = [nat_qkv[:, c, P * k:P * k + P] for k in range(KC) for c in (2 * j, 2 * j + 1)]
                else:
                    pe.wait_ge(ld["o"], 16)
                    blocks = [nat_o[:, k, P * c:P * c + P] for c in (2 * j, 2 * j + 1) for k in range(2)]
                transposes(bank[6 + n % 2], blocks).then_inc(sh_full, 1)

            W = [(0, 0), (1, 0), (0, 1)]

            def group_cols(w, k, it, what):
                g = (it + 1) // B
                if what == "q":
                    return w[:, k, bass.ds(g * (HG * DH), HG * DH)]
                kv = w[:, k, H * DH:QKV1].rearrange("p (w n) -> p w n", w=2)
                return kv[:, :, bass.ds(g * DH, DH)]

            def tokens(c, s, k, b_next):
                return xT[s][:, k, SEQ * b_next + P * c:SEQ * b_next + P * c + P]

            def project_q(c, it, kind, b_next):
                b, n = place(f"q{c}", it, kind)
                if n > 0 or kind == INNER:
                    pe.wait_ge(free[b], n)
                i = 0
                for s, w in W:
                    for k in range(KC):
                        ins = pe.matmul(bank[b][:, :], tokens(c, s, k, b_next), group_cols(qkvT[w], k, it, "q"), start=i == 0, stop=i == 5)
                        i += 1
                ins.then_inc(full[b], 1)

            def project_kv(it, kind, b_next):
                b, n = place("kv", it, kind)
                pe.wait_ge(free[b], n)
                for c in range(2):
                    i = 0
                    for s, w in W:
                        for k in range(KC):
                            ins = pe.matmul(bank[b][:, P * c:P * c + P].rearrange("p (w d) -> p w d", w=2), tokens(c, s, k, b_next),
                                            group_cols(qkvT[w], k, it, "kv"), start=i == 0, stop=i == 5)
                            i += 1
                ins.then_inc(full[b], 1)

            def turn(what, it, kind):
                b, n = place(what, it, kind)
                pe.wait_ge(free[b], n)
                if what == "kT":
                    pe.wait_ge(kn_done, it + 2)
                    blocks = [k_nat[:, s, c, :, :].rearrange("p w d -> p (w d)") for s in range(2) for c in range(2)]
                else:
                    j = int(what[2])
                    c, h = j // 2, 4 * (j % 2)
                    pe.wait_ge(qn_done, it * 2 + 2 + c + 1)
                    blocks = [q_nat[:, c, h + i, :, :].rearrange("p s d -> p (s d)") for i in range(4)]
                transposes(bank[b], blocks).then_inc(full[b], 1)

            pe.wait_ge(rel["act"], released("act", len(ORDER) - 1))
            pe.wait_ge(rel["dve"], released("dve", UNIT[("yT1", 0)]))
            def proj_T(j):
                if j == 0:
                    pe.wait_ge(tern_proj, 1)
                if j < 2:
                    pe.wait_ge(rel["dve"], released("dve", len(ORDER) - 1))
                else:
                    pe.wait_ge(proj_copied, j - 1)
                transposes(bank[4 + j % 2], [nat_proj[:, k, P * c:P * c + P] for c in (2 * j, 2 * j + 1)
                                             for k in range(2)]).then_inc(proj_full, 1)

            for step in range(STEPS):
                t = step - 3
                if step == 1:
                    pe.wait_ge(rel["dve"], released("dve", UNIT[("yT1", 1)]))
                if t == 0:
                    pe.wait_ge(proj_copied, FF // 256)
                if 0 <= t < TILES:
                    hidden_T(t, 0)
                if step < TILES:
                    fc(step)
                for n in SHADE_EARLY.get(step, ()):
                    shade_T(n)
                if step == 2:
                    proj_T(0)
                    proj_T(1)
                if 0 <= t < TILES:
                    hidden_T(t, 1)
                if t >= 1:
                    proj(t - 1)
                if step == 1:
                    y1_T(2)
                    y1_T(3)
                if step == 2:
                    proj_T(2)
                    proj_T(3)
                for n in SHADE_LATE.get(step, ()):
                    shade_T(n)
                for what, it in PREPARE_STEPS.get(step, ()):
                    kind = FIRST if it == 0 else BEFORE
                    if what == "kv":
                        project_kv(it, kind, it + 1)
                    elif what in ("q0", "q1"):
                        if it < 0:
                            pe.wait_ge(sh_done, len(SHADE))
                        project_q(int(what[1]), it, kind, it + 1)
                    else:
                        turn(what, it, kind)

            def scores(it, u, par, kind):
                if u == 0 or u == 2:
                    for b in (6, 7):
                        pe.wait_ge(free[b], (len(present(b, BEFORE)) if kind == FIRST else fills(b, it)) - (u == 0))
                if u >= 2 or kind != FIRST:
                    pe.wait_ge(s_exp, it * UNITS + u - 1)
                elif u == 0:
                    pe.wait_ge(f_gelu, TILES)
                ps = bank[u % 2]
                heads, h, keys = unit_heads(u)
                c = 1 if u >= 2 else 0
                for j in range(heads):
                    for s in range(2):
                        pe.matmul(ps[:, keys * j:keys * j + keys], qT[par][:, h + j, P * c:P * c + P], kT[par][:, s, 0:keys],
                                  start=j == 0 and s == 0, stop=False, skip_group_check=True)
                diag = ps[:, :].rearrange("p (h k) -> p h k", h=heads)[:, :, P * c:P * c + P]
                pe.matmul(diag, ident_b[:, :], mask_b[:, 0:heads, :], start=False, stop=True,
                          skip_group_check=True).then_inc(s_full, 1)

            def prob_T(it, u, early=False):
                n = it * UNITS + u
                pe.wait_ge(s_norm, n + 1)
                if not early:
                    pe.wait_ge(t_lo, n - 1)
                transposes(bank[2 + u % 2], [prob[u % 3][:, P * j:P * j + P] for j in range(4)]).then_inc(t_full, 1)

            def heads_out(it, u, par, first=False):
                n = it * UNITS + u
                pe.wait_ge(t_lo, n + 1)
                if not first:
                    pe.wait_ge(o_done, n - 1)
                elif u == 0:
                    pe.wait_ge(f_add, TILES)
                elif u == 2:
                    pe.wait_ge(o_done, 1)
                chunks = 1 if u < 2 else 2
                ps = bank[4 + u % 2][:, 0:512 // chunks]
                i = 0
                for k in range(chunks):
                    for w, s in W:
                        p = probT[u % 2][s][:, :].rearrange("p (h k q) -> p h k q", k=chunks, q=P)[:, :, k, :]
                        ins = pe.matmul(ps.rearrange("p (h q) -> p h q", q=P), v[par][:, k, w, :], p,
                                        start=i == 0, stop=i == 3 * chunks - 1)
                        i += 1
                ins.then_inc(pv_done, 1)

            def project_out(e, it, kind, par):
                b, n = place(f"wo{e}", it, kind)
                pe.wait_ge(free[b], n)
                pe.wait_ge(o_done, it * UNITS)
                g = (it - 1) // B
                i = 0
                for s, w in W:
                    for j in range(4):
                        rhs = woT[w][:, bass.ds(g * 4 + j, 1), :].rearrange("p a n -> p (a n)")
                        ins = pe.matmul(bank[b][:, 0:DIM], oT[par][s][:, j, e:e + 2 * P - 1:2], rhs, start=i == 0, stop=i == 11)
                        i += 1
                ins.then_inc(full[b], 1)

            def iteration(it, b_it, kind):
                par = b_it % 2
                for u in range(UNITS):
                    scores(it, u, par, kind)
                    if kind != LAST:
                        what = PROJECT_UNITS.get(u, "")
                        if what == "kv":
                            project_kv(it, kind, (b_it + 1) % B)
                        elif what and kind != FIRST:
                            project_q(int(what[1]), it, kind, (b_it + 1) % B)
                    if u >= 2:
                        prob_T(it, u - 2, early=kind == FIRST and u < 4)
                    elif kind != FIRST:
                        prob_T(it - 1, u + 4)
                    if u >= 3:
                        heads_out(it, u - 3, par, first=kind == FIRST)
                    elif kind != FIRST:
                        heads_out(it - 1, u + 3, 1 - par)
                    if u == 5 and kind != FIRST:
                        project_out(0, it, kind, 1 - par)
                        project_out(1, it, kind, 1 - par)
                    if kind != LAST:
                        for what in TURN_UNITS.get(u, ()):
                            turn(what, it, kind)

            pe.wait_ge(const_done, 1)
            iterations(pe, iteration)
            prob_T(ITS - 1, 4)
            heads_out(ITS - 1, 3, 1)
            prob_T(ITS - 1, 5)
            heads_out(ITS - 1, 4, 1)
            heads_out(ITS - 1, 5, 1)
            for e in range(2):
                project_out(e, ITS, AFTER, 1)


_INS = ["L0_attn_seq", "L0_attn_w_qkv", "L0_attn_w_out", "L0_attn_pm", "L0_ffn_weight", "L0_ffn_bias",
        "L1_attn_w_qkv", "L1_attn_w_o", "L1_ffn_w_fc", "L1_ffn_w_proj"]
_VECS = ["L0_ffn_ln_gamma", "L0_ffn_ln_beta", "L0_attn_w_norm"]


def kernel(**inputs):
    import concourse.bacc as bacc
    from concourse.bass_utils import run_bass_kernel_spmd

    nc = bacc.Bacc("TRN2", target_bir_lowering=False, num_devices=1)
    arrays, args = {}, []
    for name in _INS:
        a = np.ascontiguousarray(inputs[name])
        arrays[f"in_{name}_dram"] = a
        args.append(nc.dram_tensor(f"in_{name}_dram", a.shape, mybir.dt.from_np(a.dtype), kind="ExternalInput").ap())
    arrays["vec_dram"] = np.ascontiguousarray(np.stack([np.asarray(inputs[n]).reshape(KC, P) for n in _VECS]).transpose(2, 0, 1))
    args.append(nc.dram_tensor("vec_dram", (P, len(_VECS), KC), F32, kind="ExternalInput").ap())
    arrays["const_dram"] = constants()
    args.append(nc.dram_tensor("const_dram", (P, C_ALL), F32, kind="ExternalInput").ap())
    args.append(nc.dram_tensor("out_0_dram", (B, SEQ, DIM), F32, kind="ExternalOutput").ap())
    build(nc, *args)
    r = run_bass_kernel_spmd(nc, [arrays], core_ids=[0])
    return r.results[0]["out_0_dram"]
```
